# Optimizing a Trainium2 kernel written in Bass

```python
import numpy as np
import jax
import jax.numpy as jnp

def _softmax(x, axis=-1):
    return jax.nn.softmax(x, axis=axis)

def _gelu(x):
    return jax.nn.gelu(x, approximate=True)

def _silu(x):
    return jax.nn.silu(x)

def _sigmoid(x):
    return jax.nn.sigmoid(x)

def _layernorm(x, axis=-1, eps=1e-05):
    m = jnp.mean(x, axis=axis, keepdims=True)
    v = jnp.var(x, axis=axis, keepdims=True)
    return (x - m) / jnp.sqrt(v + eps)

def _scatter_add(tgt, idx, src, axis=0):
    return tgt.at[idx].add(src)

def _segment_sum(src, seg, n):
    return jax.ops.segment_sum(src, seg, n)
kernel_name = 'mk_xattn_ffn_d1_seqx_r2_4f4bd9'

def setup_inputs(seed: int=0):
    np.random.seed(seed)
    _w = jnp.asarray

    def _rec_inputs():
        import jax
        import jax.numpy as jnp
        _rk = jax.random.key(seed)
        x = -0.000125 + 0.9999 * jax.random.normal(jax.random.fold_in(_rk, 1), (8, 512, 2048), jnp.float32)
        _lenS = 512 - jax.random.randint(jax.random.fold_in(_rk, 7), (8,), 0, max(1, 512 // 4) + 1, jnp.int32)
        _lenS2 = 512 - jax.random.randint(jax.random.fold_in(_rk, 8), (8,), 0, max(1, 512 // 4) + 1, jnp.int32)
        _ctx_4096P = jax.random.normal(jax.random.fold_in(_rk, 11), (8, 16, 2048), jnp.float32)
        _ctx_4096c = jax.random.dirichlet(jax.random.fold_in(_rk, 511), 0.3 * jnp.ones((16,), jnp.float32), (8, 512))
        _ctx_4096t = jnp.einsum('bsk,bkd->bsd', _ctx_4096c, _ctx_4096P)
        _ctx_4096t = _ctx_4096t * jax.lax.rsqrt(jnp.mean(jnp.square(_ctx_4096t)) + 1e-12) * 0.953939
        ctx_4096 = -1.52775e-05 + 0.999936 * (_ctx_4096t + 0.3 * jax.random.normal(jax.random.fold_in(_rk, 611), (8, 512, 2048), jnp.float32))
        return (x, ctx_4096)
    x, ctx_4096 = _rec_inputs()

    def _L0_xattn_setup():
        import jax, jax.numpy as jnp
        import numpy as np
        H = 8
        C = 2

        def _autocorrelation(Q, K, V):
            B, L, D = Q.shape
            d = D // H
            q = Q.reshape(B, L, H, d).transpose(0, 2, 1, 3)
            k = K.reshape(B, L, H, d).transpose(0, 2, 1, 3)
            v = V.reshape(B, L, H, d).transpose(0, 2, 1, 3)
            qf = jnp.fft.fft(q, axis=2)
            kf = jnp.fft.fft(k, axis=2)
            corr = jnp.fft.ifft(qf * jnp.conj(kf), axis=2).real
            topk = int(C * np.log(L))
            w, idx = jax.lax.top_k(corr.transpose(0, 1, 3, 2), topk)
            w = jax.nn.softmax(w, axis=-1)
            pos = jnp.arange(L)[:, None]
            out = jnp.zeros_like(v)
            for i in range(topk):
                g = jnp.minimum(idx[:, :, None, :, i] + pos, L - 1)
                out = out + w[:, :, None, :, i] * jnp.take_along_axis(v, g, axis=2)
            return out.transpose(0, 2, 1, 3).reshape(B, L, D)
        key = jax.random.key(seed)
        k1, k2, k3 = jax.random.split(key, 3)
        B, L, D = (16, 256, 2048)
        Q = jax.random.normal(k1, (B, L, D), dtype=jnp.float32)
        K = jax.random.normal(k2, (B, L, D), dtype=jnp.float32)
        V = jax.random.normal(k3, (B, L, D), dtype=jnp.float32)
        return {'Q': Q, 'K': K, 'V': V}
    _L0_xattn_all = _L0_xattn_setup()
    _L0_xattn_in = {k: v for k, v in _L0_xattn_all.items() if k in ()}
    del _L0_xattn_all

    def _L0_ffn_setup():
        import jax, jax.numpy as jnp
        import numpy as np
        IN_F = 2048
        OUT_F = 2048
        RANK = 8
        NUM_EXPERTS = 64
        TOP_K = 16
        ROUTER_DIM = 16
        ALPHA = 32
        SCALING = ALPHA / TOP_K
        BOTTLENECK = NUM_EXPERTS * RANK
        key = jax.random.key(seed)
        ks = jax.random.split(key, 5)
        x = jax.random.normal(ks[0], (4, 2048, IN_F), dtype=jnp.float32)
        bound_a = float(np.sqrt(6.0 / IN_F))
        A_w = jax.random.uniform(ks[1], (BOTTLENECK, IN_F), jnp.float32, -bound_a, bound_a)
        B_w = jax.random.normal(ks[2], (OUT_F, BOTTLENECK), dtype=jnp.float32) * 0.02
        Wq_w = jax.random.normal(ks[3], (ROUTER_DIM, IN_F), dtype=jnp.float32) * 0.02
        keys = jax.random.normal(ks[4], (NUM_EXPERTS, ROUTER_DIM), dtype=jnp.float32) * 0.01
        return {'x': x, 'A_w': A_w, 'B_w': B_w, 'Wq_w': Wq_w, 'keys': keys}
    _L0_ffn_all = _L0_ffn_setup()
    _L0_ffn_in = {k: v for k, v in _L0_ffn_all.items() if k in ('A_w', 'B_w', 'Wq_w', 'keys')}
    del _L0_ffn_all
    return {'x': x, 'ctx_4096': ctx_4096, 'L0_ffn_A_w': _L0_ffn_in['A_w'], 'L0_ffn_B_w': _L0_ffn_in['B_w'], 'L0_ffn_Wq_w': _L0_ffn_in['Wq_w'], 'L0_ffn_keys': _L0_ffn_in['keys']}

def reference(x, ctx_4096, L0_ffn_A_w, L0_ffn_B_w, L0_ffn_Wq_w, L0_ffn_keys):
    import jax
    import jax.numpy as jnp

    def _L0_xattn_ref(Q, K, V):
        import jax, jax.numpy as jnp
        import numpy as np
        H = 8
        C = 2

        def _autocorrelation(Q, K, V):
            B, L, D = Q.shape
            d = D // H
            q = Q.reshape(B, L, H, d).transpose(0, 2, 1, 3)
            k = K.reshape(B, L, H, d).transpose(0, 2, 1, 3)
            v = V.reshape(B, L, H, d).transpose(0, 2, 1, 3)
            qf = jnp.fft.fft(q, axis=2)
            kf = jnp.fft.fft(k, axis=2)
            corr = jnp.fft.ifft(qf * jnp.conj(kf), axis=2).real
            topk = int(C * np.log(L))
            w, idx = jax.lax.top_k(corr.transpose(0, 1, 3, 2), topk)
            w = jax.nn.softmax(w, axis=-1)
            pos = jnp.arange(L)[:, None]
            out = jnp.zeros_like(v)
            for i in range(topk):
                g = jnp.minimum(idx[:, :, None, :, i] + pos, L - 1)
                out = out + w[:, :, None, :, i] * jnp.take_along_axis(v, g, axis=2)
            return out.transpose(0, 2, 1, 3).reshape(B, L, D)
        return _autocorrelation(Q, K, V)

    def _L0_ffn_ref(x, A_w, B_w, Wq_w, keys):
        import jax, jax.numpy as jnp
        import numpy as np
        IN_F = 2048
        OUT_F = 2048
        RANK = 8
        NUM_EXPERTS = 64
        TOP_K = 16
        ROUTER_DIM = 16
        ALPHA = 32
        SCALING = ALPHA / TOP_K
        BOTTLENECK = NUM_EXPERTS * RANK
        q = jnp.einsum('bsd,rd->bsr', x, Wq_w)
        scores = jnp.einsum('bsr,er->bse', q, keys)
        top_vals, top_idx = jax.lax.top_k(scores, TOP_K)
        top_w = jax.nn.softmax(top_vals, axis=-1)
        gate = jnp.sum(jax.nn.one_hot(top_idx, NUM_EXPERTS, dtype=top_w.dtype) * top_w[..., None], axis=-2)
        z = jnp.einsum('bsd,nd->bsn', x, A_w)
        z = z.reshape(*z.shape[:-1], NUM_EXPERTS, RANK)
        z_gated = (z * gate[..., None]).reshape(*z.shape[:-2], BOTTLENECK)
        out = jnp.einsum('bsn,on->bso', z_gated, B_w) * SCALING
        return out
    x = x + _L0_xattn_ref(_layernorm(x, axis=-1), ctx_4096, ctx_4096)
    x = x + _L0_ffn_ref(_layernorm(x, axis=-1), L0_ffn_A_w, L0_ffn_B_w, L0_ffn_Wq_w, L0_ffn_keys)
    return x

_drawn_inputs = setup_inputs


def setup_inputs(seed=0):
    import zlib

    import numpy as np

    out = dict(_drawn_inputs(seed))
    spreads = {}
    factors = {}
    for name, (base, spread) in spreads.items():
        noise = np.random.default_rng([zlib.crc32(name.encode()), seed]).standard_normal(out[name].shape)
        drawn = base * np.exp(spread * noise) if base else spread * noise
        out[name] = jnp.asarray(drawn.astype(out[name].dtype))
    for name, factor in factors.items():
        out[name] = (out[name] * factor).astype(out[name].dtype)
    return out
```

```python
from contextlib import ExitStack

import numpy as np

import concourse.bass as bass
from concourse import mybir

F32 = mybir.dt.float32
F32R = mybir.dt.float32r
ALU = mybir.AluOpType
ACT = mybir.ActivationFunctionType

B, L, D = 8, 512, 2048
P = 128
CH = 512
GPB = D // CH
GROUPS = B * GPB
LT = L // P
CT = CH // P
TOPK = 12
NEG = -3.0e38
EPS = 1e-5
NFFN, EXPERTS, RANK, RDIM, TOPE = 512, 64, 8, 16, 16
SCALING = 2.0
TOKENS = B * L
TT = TOKENS // P
KD = D // P
KN = NFFN // P


def transform_tables():
    H = L // 2
    p = np.arange(P)
    cos, sin, pi = np.cos, np.sin, np.pi

    def alt(n):
        return 1.0 - 2.0 * (n % 2)

    cyc = [2 * p, 2 * p + 1]
    neg = [8 * p + 1, 8 * p + 5]
    fwd = []
    for par in range(2):
        for fn in (cos, sin):
            for half in range(2):
                n = p + P * half
                m = fn(2 * pi * np.outer(n + 0.5, cyc[par]) / L)
                if par == 0 and fn is sin:
                    m[:, 0] = alt(n)
                fwd.append(m)
    for par in range(2):
        th = 2 * pi * np.outer(p + 0.5, neg[par]) / (2 * L)
        fwd += [cos(th), sin(th), -sin(th)]
    for half in range(2):
        m = cos(2 * pi * np.outer(p + P * half + 0.5, cyc[0]) / L)
        m[:, 0] = 0.0
        fwd.append(m)
    tau = np.arange(L)
    lags = []
    for par in range(2):
        for fn in (cos, sin):
            m = 2.0 * fn(2 * pi * np.outer(cyc[par], tau) / L) / L
            if par == 0:
                m[0] = alt(tau) / L if fn is cos else 0.0
            lags.append(m)
    wts = []
    for par in range(2):
        for fn in (cos, sin):
            for half in range(2):
                f = cyc[par].copy()
                if par == 0:
                    f[0] = H
                m = fn(2 * pi * np.outer(p + P * half, f) / L)
                if fn is cos:
                    m -= 1.0
                    if half == 0:
                        m[0] = alt(f) - 1.0
                elif half == 0:
                    m[0] = 0.0
                if par == 0 and fn is sin:
                    m[:, 0] = 0.0
                wts.append(m)
    for par in range(2):
        for fn in (cos, sin):
            for half in range(2):
                m = fn(2 * pi * np.outer(p + P * half, neg[par]) / (2 * L))
                if half == 0 and fn is sin:
                    m[0] = sin(pi * neg[par] / 2)
                wts.append(m)
    back = []
    for half in range(2):
        t = p + P * half + 0.5
        for par in range(2):
            m = 2.0 * cos(2 * pi * np.outer(cyc[par], t) / L) / (2 * L)
            if par == 0:
                m[0] /= 2
            back.append(m)
        for par in range(2):
            back.append(2.0 * sin(2 * pi * np.outer(neg[par], t) / (2 * L)) / (2 * L))
        for par in range(2):
            m = 2.0 * sin(2 * pi * np.outer(cyc[par], t) / L) / (2 * L)
            if par == 0:
                m[0] = alt(p) / (2 * L)
            back.append(m)
        for par in range(2):
            back.append(2.0 * cos(2 * pi * np.outer(neg[par], t) / (2 * L)) / (2 * L))

    def cat(ms):
        return np.ascontiguousarray(np.concatenate(ms, 1).astype(np.float32))

    return {
        "fwd": cat(fwd), "lags": cat(lags), "wts": cat(wts), "back": cat(back),
        "ident": np.eye(P, dtype=np.float32), "flip": np.ascontiguousarray(np.eye(P, dtype=np.float32)[::-1]),
    }


def attention_phase(nc, sems, x, ctx, tables, x2, rstd2, shift2):
    with ExitStack() as st:
        def sb(name, shape, dt=F32):
            return st.enter_context(nc.sbuf_tensor(name, shape, dt))

        def ps(name, shape):
            return st.enter_context(nc.psum_tensor(name, shape, F32))

        def sem(name):
            return sems.enter_context(nc.semaphore(name))

        fwd = sb("fwd", [P, 16, P])
        wts = sb("wts", [P, 16, P])
        lags_hi, lags_lo = sb("lags_hi", [P, LT, L], F32R), sb("lags_lo", [P, LT, L], F32R)
        back_hi, back_lo = sb("back_hi", [P, 16, P], F32R), sb("back_lo", [P, 16, P], F32R)
        ident, flip = sb("ident", [P, P]), sb("flip", [P, P])
        stat_in = sb("stat_in", [P, D // 2])
        bn_x, bn_x2 = sb("bn_x", [P, LT, GPB, 6]), sb("bn_x2", [P, LT, GPB, 6])
        norm_x = [sb(f"norm_x{n}", [P, LT, 2]) for n in range(4)]
        norm_x2 = [sb(f"norm_x2{n}", [P, LT, 2]) for n in range(4)]
        pace, zero = sb("pace", [P, 34]), sb("zero", [P, 1])
        rstd, shift = sb("rstd", [P, B * LT]), sb("shift", [P, B * LT])
        xq = sb("xq", [P, LT, CH])
        q_fold = sb("q_fold", [P, LT, CH])
        v = sb("v", [P, LT, CH])
        v_last = sb("v_last", [P, CH])
        v_fold = sb("v_fold", [P, LT, CH])
        v_scaled = sb("v_scaled", [P, 2, CH])
        v_spec = sb("v_spec", [P, 8, CH])
        prod = sb("prod", [P, 3, 2, CH])
        p_hi, p_lo = sb("p_hi", [P, 4, CH], F32R), sb("p_lo", [P, 4, CH], F32R)
        r_hi, r_lo = sb("r_hi", [P, 8, CH], F32R), sb("r_lo", [P, 8, CH], F32R)
        top = sb("top", [P, 2, 16])
        neg_max, exp_sum, inv_sum = sb("neg_max", [P, 2]), sb("exp_sum", [P, 2]), sb("inv_sum", [P, 2])
        exp_top = sb("exp_top", [P, 2, TOPK])
        e = sb("e", [P, 2, L])
        pick = sb("pick", [P, CT, L])
        w_t = sb("w_t", [P, LT, CH])
        xr = sb("xr", [P, LT, CH])
        rev = sb("rev", [P, 2, CH])

        pair_ps = [[ps(f"pair{s}{n}", [P, CH]) for n in "ab"] for s in range(2)]
        lag_ps = [ps(f"lag{s}", [P, L]) for s in range(2)]
        evac_ps = [ps(f"evac{s}", [P, CH]) for s in range(2)]

        tables_loaded, tables_split = sem("tables_loaded"), sem("tables_split")
        stat_loaded, stat_used = sem("stat_loaded"), sem("stat_used")
        x_norm_step, x_sqrt_done, x_norm_ready = sem("x_norm_step"), sem("x_sqrt_done"), sem("x_norm_ready")
        x2_stat, x2_norm_step, x2_sqrt_done, x2_norm_ready = (
            sem("x2_stat"), sem("x2_norm_step"), sem("x2_sqrt_done"), sem("x2_norm_ready"))
        xq_loaded, v_loaded, xr_loaded = sem("xq_loaded"), sem("v_loaded"), sem("xr_loaded")
        normed, q_folded = sem("normed"), sem("q_folded")
        v_shifted, v_folded, v_halves, v_twisted = sem("v_shifted"), sem("v_folded"), sem("v_halves"), sem("v_twisted")
        evac_ready, evac_done = sem("evac_ready"), sem("evac_done")
        pair_ready, pair_done = sem("pair_ready"), sem("pair_done")
        prod_ready, prod_added, sum_ready = sem("prod_ready"), sem("prod_added"), sem("sum_ready")
        hi_done, lo_done = sem("hi_done"), sem("lo_done")
        dc_done = sem("dc_done")
        lag_ready, topk_step, exp_done, mask_step = sem("lag_ready"), sem("topk_step"), sem("exp_done"), sem("mask_step")
        weighted, w_folded = sem("weighted"), sem("w_folded")
        even_copied, rev_ready, x2_step, flip_used, stored = (
            sem("even_copied"), sem("rev_ready"), sem("x2_step"), sem("flip_used"), sem("stored"))

        x_t = x.rearrange("b (j p) d -> b p j d", p=P)
        ctx_t = ctx.rearrange("b (j p) d -> b p j d", p=P)
        x2_t = x2.rearrange("b (j p) d -> p (b j) d", p=P)

        def at_group(arr, k, r, off):
            q = (1 + r + off) % GPB
            return arr[bass.ds(k + (1 + r + off) // GPB, 1), :, :, q * CH:(q + 1) * CH].rearrange("o p j c -> (o p) j c")

        def is_first(k):
            return isinstance(k, int) and k < 0

        def is_last(i):
            return isinstance(i, int) and i == GROUPS

        def evac_wt(i, n):
            return 12 * i - 4 + n

        def evac_v(i, n):
            return 12 * i + n

        def pair_w(i, n):
            return 8 * i - 6 + n

        def pair_q(i, n, k):
            return n if is_first(k) else 8 * i - 2 + n

        def pair_o(i, n):
            return 8 * i + n - (2 if is_last(i) else 0)

        def lag_c(i, n, k):
            return n if is_first(k) else 6 * i - 2 + n

        def lag_flip(i, n):
            return 6 * i + 2 + n - (CT if is_last(i) else 0)

        def half_r(i, n):
            return 12 * i - 8 + n

        def half_p(i, n):
            return 12 * i + n

        def steps(eng, body):
            body(-1, 3, True, False, True, False)
            with eng.Fori(0, B - 1) as k:
                for r in range(4):
                    body(k, r, True, True, True, r < 2)
            for r in range(4):
                body(B - 1, r, r < 3, True, r < 2, False)

        block = st.enter_context(nc.Block())

        @block.sync
        def _(sp):
            for dst, name in ((fwd, "fwd"), (wts, "wts"), (ident, "ident"), (flip, "flip")):
                sp.dma_start(dst[:].rearrange("p n m -> p (n m)") if dst in (fwd, wts) else dst[:],
                             tables[name]).then_inc(tables_loaded, 16)
            stage = v_spec[:].rearrange("p n c -> p (n c)")
            sp.dma_start(stage[:, 0:2048], tables["lags"]).then_inc(tables_loaded, 16)
            sp.dma_start(stage[:, 2048:4096], tables["back"]).then_inc(tables_loaded, 16)

            def stat_load(batch, tile, half, n):
                if not (isinstance(n, int) and n == 0):
                    sp.wait_ge(stat_used, n)
                sp.dma_start(stat_in[:], x[bass.ds(batch, 1), tile * P:(tile + 1) * P, half * (D // 2):(half + 1) * (D // 2)]
                             .rearrange("o p d -> (o p) d")).then_inc(stat_loaded, 16)

            def load_xq(k, r, off):
                sp.dma_start(xq[:], at_group(x_t, k, r, off)).then_inc(xq_loaded, 16)

            def load_v(k, r, off):
                q = (1 + r + off) % GPB
                sp.dma_start(v[:], at_group(ctx_t, k, r, off)).then_inc(v_loaded, 16)
                last = ctx[bass.ds(k + (1 + r + off) // GPB, 1), L - 1:L, q * CH:(q + 1) * CH].rearrange("o p c -> (o p) c")
                sp.dma_start(v_last[:], last.broadcast_to((P, CH))).then_inc(v_loaded, 16)

            load_xq(-1, 3, 0)
            load_v(-1, 3, 0)
            for n in range(2 * LT):
                stat_load(0, n // 2, n % 2, n)

            def body(k, r, a, b, f, stats):
                i = 4 * k + 1 + r
                if stats:
                    for n in range(4):
                        tile = 2 * r + n // 2
                        stat_load(k + 1, tile, n % 2, 8 * (k + 1) + 2 * tile + n % 2)
                if f:
                    sp.wait_ge(q_folded, i + 1)
                    load_xq(k, r, 1)
                    sp.wait_ge(evac_ready, evac_v(i, 7) + 1)
                    sp.wait_ge(dc_done, i + 1)
                    load_v(k, r, 1)
                if b:
                    sp.wait_ge(x2_stat, LT * i)
                    sp.dma_start(x2_t[:, bass.ds(LT * k, LT), r * CH:(r + 1) * CH], xr[:]).then_inc(stored, 16)
                    if a:
                        sp.wait_ge(stored, 16 * i)
                if a:
                    sp.dma_start(xr[:], at_group(x_t, k, r, 0)).then_inc(xr_loaded, 16)

            steps(sp, body)
            sp.wait_ge(stored, 16 * GROUPS)

        @block.tensor
        def _(pe):
            def fwd_mm(out, n, rhs, start, stop):
                return nc.tensor.matmul(out[:], fwd[:, n, :], rhs, start=start, stop=stop)

            def split_mm(out, lhs_hi, lhs_lo, rhs_hi, rhs_lo, start, stop):
                nc.tensor.matmul(out[:], lhs_hi, rhs_hi, start=start, stop=False)
                nc.tensor.matmul(out[:], lhs_hi, rhs_lo, start=False, stop=False)
                return nc.tensor.matmul(out[:], lhs_lo, rhs_hi, start=False, stop=stop)

            def evac_slot(n):
                pe.wait_ge(evac_done, n - 1) if not (isinstance(n, int) and n < 2) else None

            def products_taken(half):
                pe.wait_ge(prod_ready, half + 1)

            pe.wait_ge(tables_loaded, 16 * 6)
            pe.wait_ge(tables_split, 4)

            def body(k, r, a, b, f, stats):
                i = 4 * k + 1 + r
                if b:
                    pe.wait_ge(w_folded, 3 * CT * i)
                    for l in range(LT):
                        evac_slot(evac_wt(i, l))
                        for c in range(CT):
                            last = nc.tensor.transpose(evac_ps[l % 2][:, c * P:(c + 1) * P],
                                                       pick[:, c, l * P:(l + 1) * P], ident[:])
                        last.then_inc(evac_ready, 1)
                    pe.wait_ge(evac_done, evac_wt(i, 3) + 1)
                    for n in range(4):
                        if n >= 2:
                            products_taken(half_r(i, 2 * n - 3))
                        else:
                            pe.wait_ge(pair_done, 2 * (i - 1) + n + 1)
                        cos_in, sin_in = (0, 2) if n < 2 else (2, 0)
                        bank = pair_ps[n % 2]
                        for h in range(2):
                            nc.tensor.matmul(bank[0][:], wts[:, 4 * n + h, :], w_t[:, cos_in + h, :],
                                             start=h == 0, stop=h == 1)
                        for h in range(2):
                            last = nc.tensor.matmul(bank[1][:], wts[:, 4 * n + 2 + h, :], w_t[:, sin_in + h, :],
                                                    start=h == 0, stop=h == 1)
                        last.then_inc(pair_ready, 1)
                if a:
                    pe.wait_ge(v_folded, 2 * i + 2)
                    for n in range(4):
                        evac_slot(evac_v(i, n))
                        bank = evac_ps[n % 2]
                        for h in range(2):
                            last = fwd_mm(bank, 2 * n + h, v_fold[:, 2 * (n // 2) + h, :], h == 0, h == 1)
                        last.then_inc(evac_ready, 1)
                    pe.wait_ge(q_folded, i + 1)
                    for n in range(2):
                        if b:
                            products_taken(half_r(i, 5 + 2 * n))
                        bank = pair_ps[n % 2]
                        for h in range(2):
                            fwd_mm(bank[0], 14 + h if n == 0 else 4 + h, q_fold[:, 2 * n + h, :], h == 0, h == 1)
                        for h in range(2):
                            last = fwd_mm(bank[1], 4 * n + 2 + h, q_fold[:, 2 * n + h, :], h == 0, h == 1)
                        last.then_inc(pair_ready, 1)
                    pe.wait_ge(v_twisted, 4 * i + 4)
                    for n in range(4):
                        evac_slot(evac_v(i, 4 + n))
                        bank = evac_ps[n % 2]
                        re, im = (1, 3) if n < 2 else (0, 2)
                        t = 8 + 3 * (n // 2)
                        fwd_mm(bank, t + (n % 2), v[:, re, :], True, False)
                        fwd_mm(bank, t + (2 if n % 2 == 0 else 0), v[:, im, :], False, True).then_inc(evac_ready, 1)
                    pe.wait_ge(hi_done, half_p(i, 3) + 1)
                    pe.wait_ge(lo_done, half_p(i, 3) + 1)
                    for c in range(CT):
                        if c < 2 and b:
                            pe.wait_ge(flip_used, 2 * i)
                            pe.wait_ge(topk_step, 24 * (i - 1) + 6 * (c + 2) + 3)
                            pe.wait_ge(exp_done, 8 * (i - 1) + 2 * (c + 2) + 1)
                        elif c >= 2:
                            pe.wait_ge(topk_step, 24 * i + 6 * (c - 2) + 3)
                            pe.wait_ge(exp_done, 8 * i + 2 * (c - 2) + 1)
                        for n in range(4):
                            cols = slice(c * P, (c + 1) * P)
                            last = split_mm(lag_ps[c % 2], p_hi[:, n, cols], p_lo[:, n, cols],
                                            lags_hi[:, n, :], lags_lo[:, n, :], n == 0, n == 3)
                        last.then_inc(lag_ready, 1)
                if b:
                    pe.wait_ge(hi_done, half_r(i, 7) + 1)
                    pe.wait_ge(lo_done, half_r(i, 7) + 1)
                    for h in range(2):
                        products_taken(half_p(i, 2 * h + 1) if a else half_r(i, 5 + 2 * h))
                        for part, rows in enumerate(((0, 2, 5, 7), (1, 3, 4, 6))):
                            for n, row in enumerate(rows):
                                t = 8 * h + 4 * part + n
                                last = split_mm(pair_ps[h][part], back_hi[:, t, :], back_lo[:, t, :],
                                                r_hi[:, row, :], r_lo[:, row, :], n == 0, n == 3)
                        last.then_inc(pair_ready, 1)
                    for h in range(2):
                        if a:
                            pe.wait_ge(topk_step, 24 * i + 6 * (2 + h) + 3)
                            pe.wait_ge(exp_done, 8 * i + 2 * (2 + h) + 1)
                        else:
                            pe.wait_ge(flip_used, 2 * i + h - 1)
                        pe.wait_ge(rev_ready, 2 * (i - 1) + h + 1)
                        nc.tensor.matmul(lag_ps[h][:], flip[:], rev[:, h, :], start=True, stop=True).then_inc(lag_ready, 1)

            steps(pe, body)

        @block.vector
        def _(dve):
            dve.wait_ge(tables_loaded, 16 * 6)
            stage = v_spec[:].rearrange("p n c -> p (n c)")
            dve.wait_ge(tables_split, 2)
            nc.vector.tensor_tensor(lags_lo[:].rearrange("p n c -> p (n c)"), stage[:, 0:2048],
                                    lags_hi[:].rearrange("p n c -> p (n c)").bitcast(F32), ALU.subtract).then_inc(tables_split, 1)
            nc.vector.tensor_tensor(back_lo[:].rearrange("p n c -> p (n c)"), stage[:, 2048:4096],
                                    back_hi[:].rearrange("p n c -> p (n c)").bitcast(F32), ALU.subtract).then_inc(tables_split, 1)

            held = [0]

            def hold(sem, value):
                dve.wait_ge(sem, value)
                nc.vector.memset(pace[:, held[0] % 32:held[0] % 32 + 1], 0.0)
                held[0] += 1

            def half_tile_stats(tile, half, n):
                dve.wait_ge(stat_loaded, 16 * n + 16)
                for h in range(2):
                    op = nc.vector.bn_stats(bn_x[:, tile, 2 * half + h, :], stat_in[:, h * CH:(h + 1) * CH])
                op.then_inc(stat_used, 1)

            def norm_begin(bn, tmp, step, n):
                mv, ve = tmp[0], tmp[1]
                for j in range(LT):
                    nc.vector.bn_aggr(mv[:, j, :], bn[:, j, :, :].rearrange("p g s -> p (g s)")).then_inc(step, 1)
                dve.wait_ge(step, 9 * n + 4)
                nc.vector.tensor_scalar(ve[:, :, 0], mv[:, :, 1], EPS, None, ALU.add).then_inc(step, 1)

            def norm_end(tmp, step, sqrt_done, n, scale, shift_, ready):
                mv, ve, sd, t = tmp
                y0, t = sd[:, :, 1], t[:, :, 0]
                cols = bass.ds(LT * n, LT)
                dve.wait_ge(sqrt_done, n + 1)
                nc.vector.reciprocal(y0, sd[:, :, 0]).then_inc(step, 1)
                dve.wait_ge(step, 9 * n + 6)
                nc.vector.tensor_tensor(t, ve[:, :, 0], y0, ALU.mult).then_inc(step, 1)
                dve.wait_ge(step, 9 * n + 7)
                nc.vector.tensor_tensor(t, t, y0, ALU.mult).then_inc(step, 1)
                dve.wait_ge(step, 9 * n + 8)
                nc.vector.tensor_scalar(t, t, -0.5, 1.5, ALU.mult, ALU.add).then_inc(step, 1)
                dve.wait_ge(step, 9 * n + 9)
                nc.vector.tensor_tensor(scale[:, cols], t, y0, ALU.mult).then_inc(ready, 1)
                dve.wait_ge(ready, 2 * n + 1)
                nc.vector.scalar_tensor_tensor(shift_[:, cols], mv[:, :, 0], -1.0, scale[:, cols],
                                               ALU.mult, ALU.mult).then_inc(ready, 1)

            def low_half(n, buf, slot, row):
                dve.wait_ge(hi_done, n + 1)
                nc.vector.tensor_tensor(buf[:, row, :], prod[:, slot, 0, :],
                                        (p_hi if buf is p_lo else r_hi)[:, row, :].bitcast(F32), ALU.subtract).then_inc(lo_done, 1)

            def products(count, half, slot_of, pair, buf, spec_wait, plus_one):
                for n in range(count):
                    blk = n // 2
                    c_ps, s_ps = pair_ps[blk % 2]
                    c_v, s_v = v_spec[:, 2 * blk, :], v_spec[:, 2 * blk + 1, :]
                    if n % 2 == 0:
                        dve.wait_ge(pair_ready, pair(blk) + 1)
                        spec_wait(blk)
                    slot = slot_of(n)
                    if not (isinstance(half(n), int) and half(n) < 3):
                        dve.wait_ge(lo_done, half(n) - 2)
                    first_v, second_v = (c_v, s_v) if n % 2 == 0 else (s_v, c_v)
                    if plus_one is None and n % 2 == 1:
                        nc.vector.tensor_tensor(prod[:, slot, 0, :], s_ps[:], c_v, ALU.mult)
                        op = nc.vector.tensor_tensor(prod[:, slot, 1, :], c_ps[:], s_v, ALU.mult)
                    else:
                        if plus_one and blk < 2:
                            nc.vector.scalar_tensor_tensor(prod[:, slot, 0, :], c_ps[:], 1.0, first_v, ALU.add, ALU.mult)
                        else:
                            nc.vector.tensor_tensor(prod[:, slot, 0, :], c_ps[:], first_v, ALU.mult)
                        op = nc.vector.tensor_tensor(prod[:, slot, 1, :], s_ps[:], second_v, ALU.mult)
                    op.then_inc(prod_ready, 1)
                    if n >= 2:
                        low_half(half(n - 2), buf, slot_of(n - 2), n - 2)
                for n in range(count - 2, count):
                    low_half(half(n), buf, slot_of(n), n)

            for n in range(2 * LT):
                half_tile_stats(n // 2, n % 2, n)
            dve.wait_ge(stat_used, 2 * LT)
            norm_begin(bn_x, norm_x, x_norm_step, 0)
            norm_end(norm_x, x_norm_step, x_sqrt_done, 0, rstd, shift, x_norm_ready)

            def body(k, r, a, b, f, stats):
                i = 4 * k + 1 + r
                if b:
                    dve.wait_ge(dc_done, i)
                    products(8, lambda n: half_r(i, n), lambda n: (n + 1) % 3, lambda n: pair_w(i, n), r_lo,
                             lambda blk: None, True)
                if stats:
                    for n in range(4):
                        tile = 2 * r + n // 2
                        half_tile_stats(tile, n % 2, 8 * (k + 1) + 2 * tile + n % 2)
                    if r == 1:
                        hold(stat_used, 8 * (k + 1) + 8)
                        norm_begin(bn_x, norm_x, x_norm_step, k + 1)
                if a:
                    products(4, lambda n: half_p(i, n), lambda n: n % 3, lambda n: pair_q(i, n, k), p_lo,
                             lambda blk: dve.wait_ge(evac_done, evac_v(i, 2 * blk + 1) + 1), None)
                    if not b:
                        dve.wait_ge(prod_ready, half_p(i, 3) + 1)
                        nc.vector.memset(pace[:, 32:33], 0.0).then_inc(pair_done, 2)
                        nc.vector.memset(pace[:, 33:34], 0.0).then_inc(flip_used, 2)
                    if stats and r == 1:
                        norm_end(norm_x, x_norm_step, x_sqrt_done, k + 1, rstd, shift, x_norm_ready)
                    dve.wait_ge(prod_ready, half_p(i, 0) + 1)
                    nc.vector.scalar_tensor_tensor(v_spec[0:1, 0, :], v_last[0:1, :], float(2 * L), v_spec[0:1, 0, :],
                                                   ALU.mult, ALU.add).then_inc(dc_done, 1)

                    def finish_mask(c):
                        n = CT * i + c
                        s = c % 2
                        dve.wait_ge(exp_done, 2 * n + 2)
                        nc.vector.reciprocal(inv_sum[:, s:s + 1], exp_sum[:, s:s + 1]).then_inc(mask_step, 1)
                        dve.wait_ge(mask_step, 2 * n + 1)
                        dve.wait_ge(topk_step, 6 * n + 6)
                        nc.vector.tensor_scalar(pick[:, c, :], pick[:, c, :], NEG, inv_sum[:, s:s + 1],
                                                ALU.is_equal, ALU.mult).then_inc(mask_step, 1)

                    if b:
                        dve.wait_ge(evac_ready, evac_wt(i, 3) + 1)
                    for c in range(CT):
                        n = CT * i + c
                        s = c % 2
                        corr = lag_ps[s]
                        hold(lag_ready, lag_c(i, c, k) + 1)
                        if not (isinstance(n, int) and n < 2):
                            hold(exp_done, 2 * n - 2)
                        nc.vector.max(top[:, s, 0:8], corr[:]).then_inc(topk_step, 1)
                        dve.wait_ge(topk_step, 6 * n + 1)
                        nc.vector.tensor_scalar(neg_max[:, s:s + 1], top[:, s, 0:1], -1.0, None, ALU.mult).then_inc(topk_step, 1)
                        nc.vector.match_replace(pick[:, c, :], top[:, s, 0:8], corr[:], NEG).then_inc(topk_step, 1)
                        hold(topk_step, 6 * n + 3)
                        nc.vector.max(top[:, s, 8:16], pick[:, c, :]).then_inc(topk_step, 1)
                        dve.wait_ge(topk_step, 6 * n + 4)
                        nc.vector.memset(top[:, s, TOPK:16], NEG).then_inc(topk_step, 1)
                        hold(topk_step, 6 * n + 5)
                        nc.vector.match_replace(pick[:, c, :], top[:, s, 8:16], pick[:, c, :], NEG).then_inc(topk_step, 1)
                        if c:
                            finish_mask(c - 1)
                    finish_mask(CT - 1)
                if b:
                    dve.wait_ge(xr_loaded, 16 * i)
                    for h in range(2):
                        n = 2 * (i - 1) + h
                        even, odd = pair_ps[h]
                        dve.wait_ge(pair_ready, pair_o(i, h) + 1)
                        dve.wait_ge(even_copied, n + 1)
                        nc.vector.tensor_tensor(xr[:, h, :], even[:], xr[:, h, :], ALU.add).then_inc(x2_step, 1)
                        nc.vector.tensor_tensor(rev[:, h, :], rev[:, h, :], odd[:], ALU.subtract).then_inc(rev_ready, 1)
                        dve.wait_ge(x2_step, n + 1)
                        nc.vector.tensor_tensor(xr[:, h, :], odd[:], xr[:, h, :], ALU.add).then_inc(pair_done, 1)
                    for h in range(2):
                        dve.wait_ge(lag_ready, lag_flip(i, h) + 1)
                        nc.vector.tensor_tensor(xr[:, 3 - h, :], lag_ps[h][:], xr[:, 3 - h, :], ALU.add).then_inc(flip_used, 1)
                    dve.wait_ge(pair_done, 2 * i + 2)
                    for j in range(LT):
                        if j == 2:
                            dve.wait_ge(flip_used, 2 * i + 2)
                        nc.vector.bn_stats(bn_x2[:, j, r, :], xr[:, j, :]).then_inc(x2_stat, 1)
                    if r == 3:
                        hold(x2_stat, LT * i)
                        norm_begin(bn_x2, norm_x2, x2_norm_step, k)
                        norm_end(norm_x2, x2_norm_step, x2_sqrt_done, k, rstd2, shift2, x2_norm_ready)

            steps(dve, body)

        @block.scalar
        def _(act):
            stage = v_spec[:].rearrange("p n c -> p (n c)")
            act.wait_ge(tables_loaded, 16 * 6)
            nc.scalar.activation(lags_hi[:].rearrange("p n c -> p (n c)"), stage[:, 0:2048], ACT.Copy).then_inc(tables_split, 1)
            nc.scalar.activation(back_hi[:].rearrange("p n c -> p (n c)"), stage[:, 2048:4096], ACT.Copy).then_inc(tables_split, 1)

            def norm_inputs(k, r, off):
                act.wait_ge(xq_loaded, 16 * (4 * k + 1 + r + off) + 16)
                act.wait_ge(x_norm_ready, 2 * (k + (1 + r + off) // GPB) + 2)

            def norm(k, r, off):
                batch = k + (1 + r + off) // GPB
                for j in range(LT):
                    t = bass.ds(LT * batch + j, 1)
                    nc.scalar.activation(xq[:, j, :], xq[:, j, :], ACT.Identity, bias=shift[:, t], scale=rstd[:, t]).then_inc(normed, 1)

            def halves(g):
                act.wait_ge(v_folded, 2 * g + 2)
                for n, src in enumerate((3, 1)):
                    nc.scalar.activation(v_scaled[:, n, :], v_fold[:, src, :], ACT.Copy, scale=0.5 ** 0.5).then_inc(v_halves, 1)

            def high_half(n, buf, slot, row):
                act.wait_ge(sum_ready, n + 1)
                nc.scalar.activation(buf[:, row, :], prod[:, slot, 0, :], ACT.Copy).then_inc(hi_done, 1)

            def evac(n, dst, src):
                act.wait_ge(evac_ready, n + 1)
                nc.scalar.activation(dst, src[:], ACT.Copy).then_inc(evac_done, 1)

            def sqrt(tmp, step, done, n):
                act.wait_ge(step, 9 * n + 5)
                nc.scalar.activation(tmp[2][:, :, 0], tmp[1][:, :, 0], ACT.Sqrt).then_inc(done, 1)

            sqrt(norm_x, x_norm_step, x_sqrt_done, 0)
            norm_inputs(-1, 3, 0)
            norm(-1, 3, 0)
            halves(0)

            def body(k, r, a, b, f, stats):
                i = 4 * k + 1 + r
                if b:
                    for l in range(LT):
                        evac(evac_wt(i, l), w_t[:, l, :], evac_ps[l % 2])
                    if not (isinstance(i, int) and i < 2):
                        act.wait_ge(pair_ready, pair_o(i - 1, 1) + 1)
                    for n in range(8):
                        high_half(half_r(i, n), r_hi, (n + 1) % 3, n)
                if a:
                    for n in range(8):
                        if b and n % 2 == 0:
                            act.wait_ge(prod_ready, half_r(i, n + 1) + 1)
                        elif n == 0:
                            act.wait_ge(tables_split, 4)
                        if n == 3 and f:
                            norm_inputs(k, r, 1)
                        evac(evac_v(i, n), v_spec[:, n, :], evac_ps[n % 2])
                        if n == 3:
                            if stats and r == 1:
                                sqrt(norm_x, x_norm_step, x_sqrt_done, k + 1)
                            if f:
                                norm(k, r, 1)
                        if n >= 4:
                            high_half(half_p(i, n - 4), p_hi, (n - 4) % 3, n - 4)
                    for c in range(CT):
                        n = CT * i + c
                        s = c % 2
                        act.wait_ge(topk_step, 6 * n + 3)
                        if not (isinstance(n, int) and n < 2):
                            act.wait_ge(w_folded, 3 * (n - 1))
                        nc.scalar.activation(e[:, s, :], lag_ps[s][:], ACT.Exp, bias=neg_max[:, s:s + 1]).then_inc(exp_done, 1)
                        act.wait_ge(topk_step, 6 * n + 4)
                        if not (isinstance(n, int) and n < 2):
                            act.wait_ge(mask_step, 2 * (n - 2) + 1)
                        nc.scalar.activation(exp_top[:, s, :], top[:, s, 0:TOPK], ACT.Exp, bias=neg_max[:, s:s + 1],
                                             accum_out=exp_sum[:, s:s + 1]).then_inc(exp_done, 1)
                if f:
                    halves(i + 1)
                if b:
                    for h in range(2):
                        act.wait_ge(pair_ready, pair_o(i, h) + 1)
                        if not (isinstance(i, int) and i < 2):
                            act.wait_ge(lag_ready, lag_flip(i - 1, h) + 1)
                        nc.scalar.activation(rev[:, h, :], pair_ps[h][0][:], ACT.Copy).then_inc(even_copied, 1)
                    if r == 3:
                        sqrt(norm_x2, x2_norm_step, x2_sqrt_done, k)

            steps(act, body)

        @block.gpsimd
        def _(pool):
            def fold_q(g, used):
                pool.wait_ge(normed, LT * g + LT)
                used()
                nc.gpsimd.tensor_tensor(q_fold[:, 0:2, :], xq[:, 0:2, :], xq[:, 2:4, :], ALU.add)
                nc.gpsimd.tensor_tensor(q_fold[:, 2:4, :], xq[:, 0:2, :], xq[:, 2:4, :], ALU.subtract).then_inc(q_folded, 1)

            def shift_v(g):
                pool.wait_ge(v_loaded, 32 * g + 32)
                nc.gpsimd.tensor_tensor(v[:], v[:], v_last[:].unsqueeze(1).broadcast_to((P, LT, CH)), ALU.subtract).then_inc(v_shifted, 1)

            def fold_v(g):
                pool.wait_ge(v_shifted, g + 1)
                nc.gpsimd.tensor_tensor(v_fold[:, 0:2, :], v[:, 0:2, :], v[:, 2:4, :], ALU.add).then_inc(v_folded, 1)
                nc.gpsimd.tensor_tensor(v_fold[:, 2:4, :], v[:, 0:2, :], v[:, 2:4, :], ALU.subtract).then_inc(v_folded, 1)

            def twist_v(g):
                pool.wait_ge(v_folded, 2 * g + 2)
                pool.wait_ge(v_halves, 2 * g + 2)
                for n in range(2):
                    nc.gpsimd.tensor_tensor(v[:, 2 * n + 1, :], v[:, 2 * n, :], v_scaled[:, n, :], ALU.add).then_inc(v_twisted, 1)
                for n in range(2):
                    nc.gpsimd.tensor_tensor(v[:, 2 * n, :], v[:, 2 * n, :], v_scaled[:, n, :], ALU.subtract).then_inc(v_twisted, 1)

            def add_half(n, slot, op, dc):
                pool.wait_ge(prod_ready, n + 1)
                ins = nc.gpsimd.tensor_tensor(prod[:, slot, 0, :], prod[:, slot, 0, :], prod[:, slot, 1, :], op)
                if dc is not None:
                    ins.then_inc(prod_added, 1)
                    pool.wait_ge(prod_added, dc)
                    row = v_spec[0:1, 0, :]
                    ins = nc.gpsimd.tensor_tensor(prod[0:1, slot, 0, :], row, zero[0:1, :].broadcast_to((1, CH)), ALU.add)
                ins.then_inc(sum_ready, 1)

            nc.gpsimd.memset(zero[:], 0.0).then_inc(prod_added, 1)
            fold_q(0, lambda: None)
            shift_v(0)
            fold_v(0)
            twist_v(0)

            def body(k, r, a, b, f, stats):
                i = 4 * k + 1 + r
                if b:
                    for n in range(8):
                        add_half(half_r(i, n), (n + 1) % 3, ALU.add if n % 2 == 0 else ALU.subtract, i + 1 if n == 0 else None)
                if a:
                    for n in range(4):
                        add_half(half_p(i, n), n % 3, ALU.add if n % 2 == 0 else ALU.subtract, None)
                if f:
                    fold_q(i + 1, lambda: pool.wait_ge(pair_ready, pair_q(i, 1, k) + 1))

                def weights(c):
                    n = CT * i + c
                    s = c % 2
                    pool.wait_ge(mask_step, 2 * n + 2)
                    nc.gpsimd.tensor_tensor(e[:, s, :], e[:, s, :], pick[:, c, :], ALU.mult).then_inc(weighted, 1)
                    pool.wait_ge(weighted, n + 1)
                    rev_w = e[:, s, L - 1:L // 2:-1]
                    nc.gpsimd.tensor_tensor(pick[:, c, 1:L // 2], e[:, s, 1:L // 2], rev_w, ALU.add).then_inc(w_folded, 1)
                    nc.gpsimd.tensor_tensor(pick[:, c, L // 2 + 1:L], e[:, s, 1:L // 2], rev_w, ALU.subtract).then_inc(w_folded, 1)
                    nc.gpsimd.tensor_copy(pick[:, c, 0:L:L // 2], e[:, s, L // 2::-(L // 2)]).then_inc(w_folded, 1)

                if a:
                    weights(0)
                if f:
                    shift_v(i + 1)
                if a:
                    weights(1)
                if f:
                    fold_v(i + 1)
                if a:
                    weights(2)
                    weights(3)
                if f:
                    twist_v(i + 1)

            steps(pool, body)


def ffn_phase(nc, sems, x2, a_w, b_w, wq_w, keys, tables, rstd2, shift2, out):
    with ExitStack() as st:
        def sb(name, shape, dt=F32):
            return st.enter_context(nc.sbuf_tensor(name, shape, dt))

        def ps(name, shape):
            return st.enter_context(nc.psum_tensor(name, shape, F32))

        def sem(name):
            return sems.enter_context(nc.semaphore(name))

        RING = 4
        a_hi, a_lo = sb("a_hi", [P, KD, NFFN], F32R), sb("a_lo", [P, KD, NFFN], F32R)
        b_hi, b_lo = sb("b_hi", [P, KN, D], F32R), sb("b_lo", [P, KN, D], F32R)
        wqk_hi, wqk_lo = sb("wqk_hi", [P, KD, EXPERTS], F32R), sb("wqk_lo", [P, KD, EXPERTS], F32R)
        ident2, keys_sb, keys_t = sb("ident2", [P, P]), sb("keys_sb", [EXPERTS, RDIM]), sb("keys_t", [RDIM, EXPERTS])
        rows = [sb(f"rows{n}", [P, D]) for n in range(RING)]
        xn = sb("xn", [P, D])
        xt_hi, xt_lo = sb("xt_hi", [P, KD, P], F32R), sb("xt_lo", [P, KD, P], F32R)
        zg = sb("zg", [P, NFFN])
        zt_hi, zt_lo = sb("zt_hi", [P, KN, P], F32R), sb("zt_lo", [P, KN, P], F32R)
        best, best_neg, best_exp = sb("best", [P, TOPE]), sb("best_neg", [P, 1]), sb("best_exp", [P, TOPE])
        gate_sum, gate_inv = sb("gate_sum", [P, 1]), sb("gate_inv", [P, 1])
        rest, score_exp, gate = sb("rest", [P, EXPERTS]), sb("score_exp", [P, EXPERTS]), sb("gate", [P, EXPERTS])
        pace2 = sb("pace2", [P, 32])

        tp_ps = [ps(f"tp{n}", [P, 4, P]) for n in range(2)]
        z_ps, sc_ps, zt_ps = ps("z", [P, NFFN]), ps("scores", [P, NFFN]), ps("zt", [P, KN, P])
        out_ps = [ps(f"out{n}", [P, 512]) for n in range(2)]

        small_loaded, out_stored = sem("small_loaded"), sem("out_stored")
        rows_loaded = [sem(f"rows_loaded{n}") for n in range(RING)]
        keys_turned, keys_copied, wqk_hi_done = sem("keys_turned"), sem("keys_copied"), sem("wqk_hi_done")
        xn_ready, tp_ready, tp_hi, tp_lo = sem("xn_ready"), sem("tp_ready"), sem("tp_hi"), sem("tp_lo")
        sc_ready, route_step, gate_exp = sem("sc_ready"), sem("route_step"), sem("gate_exp")
        gate_step, gate_ready = sem("gate_step"), sem("gate_ready")
        z_ready, zg_ready, zt_ready, zt_hi_done, zt_lo_done = (
            sem("z_ready"), sem("zg_ready"), sem("zt_ready"), sem("zt_hi_done"), sem("zt_lo_done"))
        out_ready, out_taken = sem("out_ready"), sem("out_taken")

        STAGES = 2 * KN
        x2_rows = x2.rearrange("b l d -> (b l) d").rearrange("(t p) d -> t p d", p=P)
        out_rows = out.rearrange("b l d -> (b l) d").rearrange("(t p) d -> t p d", p=P)
        b_rows = b_w.rearrange("(s t p) n -> s p t n", p=P, t=KN)

        def part_of_weights(w, s, q):
            a_t, b_t = w
            if s < KN:
                return a_t[:, 4 * q:4 * q + 4, s * P:(s + 1) * P]
            col = (4 * (s - KN) + q) * P
            return b_t[:, :, col:col + P]

        def tp_stage(s, q):
            return 4 * s + q

        def tp_tile(t, q):
            return 4 * (STAGES + t) + q

        def wait_rows(eng, k, n):
            eng.wait_ge(rows_loaded[n % RING], 16 * (k + n // RING + 1))

        def out_place(t, q):
            return 2 + 4 * t + q

        def steps(body):
            def run(eng):
                body(-1, 2, False, False, True)
                body(-1, 3, True, False, True)
                with eng.Fori(0, TT // RING - 1) as k:
                    for r in range(RING):
                        body(k, r, True, True, True)
                for r in range(RING):
                    body(TT // RING - 1, r, r < 3, True, r < 2)
            return run

        block = st.enter_context(nc.Block())

        @block.sync
        def _(sp):
            sp.dma_start(ident2[:], tables["ident"]).then_inc(small_loaded, 16)
            sp.dma_start(keys_sb[:], keys).then_inc(small_loaded, 16)
            for s in range(STAGES + RING):
                if s >= RING:
                    sp.wait_ge(tp_ready, tp_stage(s - RING, 3) + 1)
                buf = rows[s % RING]
                if s < KN:
                    sp.dma_start(buf[:], a_w[s * P:(s + 1) * P, :]).then_inc(rows_loaded[s % RING], 16)
                elif s < STAGES:
                    sp.dma_start(buf[:].rearrange("p (t n) -> p t n", t=KN), b_rows[s - KN]).then_inc(rows_loaded[s % RING], 16)
                else:
                    sp.dma_start(buf[:], x2_rows[s - STAGES]).then_inc(rows_loaded[s % RING], 16)
                if s == 0:
                    sp.dma_start(xn[0:RDIM, :], wq_w).then_inc(small_loaded, 16)

            def body(k, r, a, b, f):
                u = RING * k + 1 + r
                if b:
                    sp.wait_ge(out_taken, out_place(u - 1, 3) + 1)
                    sp.dma_start(out_rows[bass.ds(u - 1, 1)].rearrange("o p d -> (o p) d"), rows[r][:]).then_inc(out_stored, 16)
                if b and not isinstance(k, int):
                    sp.wait_ge(out_stored, 16 * u)
                    sp.dma_start(rows[r][:], x2_rows[bass.ds(u + 3, 1)].rearrange("o p d -> (o p) d")).then_inc(rows_loaded[r], 16)

            steps(body)(sp)
            sp.wait_ge(out_stored, 16 * TT)

        @block.tensor
        def _(pe):
            def split_mm(dst, lhs_hi, lhs_lo, rhs_hi, rhs_lo, start, stop):
                nc.tensor.matmul(dst, lhs_hi, rhs_hi, start=start, stop=False)
                nc.tensor.matmul(dst, lhs_hi, rhs_lo, start=False, stop=False)
                return nc.tensor.matmul(dst, lhs_lo, rhs_hi, start=False, stop=stop)

            def transposes(n, q, src):
                if not (isinstance(n, int) and n < 2):
                    pe.wait_ge(tp_lo, n - 1)
                for m in range(4):
                    last = nc.tensor.transpose(tp_ps[q % 2][:, m, :], src[:, (4 * q + m) * P:(4 * q + m + 1) * P], ident2[:])
                last.then_inc(tp_ready, 1)

            pe.wait_ge(small_loaded, 16 * 3)
            nc.tensor.transpose(zt_ps[0:RDIM, 0, 0:EXPERTS], keys_sb[:], ident2[0:EXPERTS, 0:EXPERTS]).then_inc(keys_turned, 1)
            pe.wait_ge(keys_copied, 1)
            for h in range(2):
                for m in range(KD // 2):
                    kt = h * (KD // 2) + m
                    last = nc.tensor.matmul(out_ps[h][:, m * EXPERTS:(m + 1) * EXPERTS], xn[0:RDIM, kt * P:(kt + 1) * P],
                                            keys_t[:], start=True, stop=True)
                last.then_inc(out_ready, 1)
            for s in range(STAGES):
                wait_rows(pe, 0, s)
                for q in range(4):
                    transposes(tp_stage(s, q), q, rows[s % RING])

            def body(k, r, a, b, f):
                u = RING * k + 1 + r
                if a:
                    pe.wait_ge(tp_hi, tp_tile(u, 3) + 1)
                    pe.wait_ge(tp_lo, tp_tile(u, 3) + 1)
                    if b:
                        pe.wait_ge(gate_ready, u)
                    else:
                        pe.wait_ge(wqk_hi_done, 2)
                        pe.wait_ge(out_taken, 2)
                    for kt in range(KD):
                        last = split_mm(sc_ps[:, 0:EXPERTS], xt_hi[:, kt, :], xt_lo[:, kt, :],
                                        wqk_hi[:, kt, :], wqk_lo[:, kt, :], kt == 0, kt == KD - 1)
                    last.then_inc(sc_ready, 1)
                if b:
                    pe.wait_ge(zg_ready, u)
                    for m in range(KN):
                        last = nc.tensor.transpose(zt_ps[:, m, :], zg[:, m * P:(m + 1) * P], ident2[:])
                    last.then_inc(zt_ready, 1)
                if a:
                    for kt in range(KD):
                        last = split_mm(z_ps[:], xt_hi[:, kt, :], xt_lo[:, kt, :], a_hi[:, kt, :], a_lo[:, kt, :],
                                        kt == 0, kt == KD - 1)
                    last.then_inc(z_ready, 1)

                def tile_transposes(q):
                    if f:
                        if q == 0:
                            pe.wait_ge(xn_ready, u + 2)
                        transposes(tp_tile(u + 1, q), q, xn)

                def out_bank(q):
                    if b:
                        pe.wait_ge(out_taken, out_place(u - 1, q) - 1)
                        for m in range(KN):
                            cols = slice(q * 512, (q + 1) * 512)
                            last = split_mm(out_ps[q % 2][:], zt_hi[:, m, :], zt_lo[:, m, :],
                                            b_hi[:, m, cols], b_lo[:, m, cols], m == 0, m == KN - 1)
                        last.then_inc(out_ready, 1)

                tile_transposes(0)
                tile_transposes(1)
                if b:
                    pe.wait_ge(zt_hi_done, u)
                    pe.wait_ge(zt_lo_done, u)
                out_bank(0)
                tile_transposes(2)
                out_bank(1)
                tile_transposes(3)
                out_bank(2)
                out_bank(3)

            steps(body)(pe)

        @block.vector
        def _(dve):
            held = [0]

            def hold(sem_, value):
                dve.wait_ge(sem_, value)
                nc.vector.memset(pace2[:, held[0] % 32:held[0] % 32 + 1], 0.0)
                held[0] += 1

            def low(n, dst, hi, src):
                dve.wait_ge(tp_hi, n + 1)
                nc.vector.tensor_tensor(dst, src[:], hi.bitcast(F32), ALU.subtract).then_inc(tp_lo, 1)

            dve.wait_ge(keys_turned, 1)
            nc.vector.tensor_copy(keys_t[:], zt_ps[0:RDIM, 0, 0:EXPERTS]).then_inc(keys_copied, 1)
            for h in range(2):
                dve.wait_ge(wqk_hi_done, h + 1)
                part = slice(h * (KD // 2), (h + 1) * (KD // 2))
                nc.vector.tensor_tensor(wqk_lo[:, part, :], out_ps[h][:].rearrange("p (m e) -> p m e", e=EXPERTS),
                                        wqk_hi[:, part, :].bitcast(F32), ALU.subtract).then_inc(out_taken, 1)
            for s in range(STAGES):
                for q in range(4):
                    hi, lo = (part_of_weights(w, s, q) for w in ((a_hi, b_hi), (a_lo, b_lo)))
                    low(tp_stage(s, q), lo, hi, tp_ps[q % 2])

            def body(k, r, a, b, f):
                u = RING * k + 1 + r
                if b:
                    dve.wait_ge(zt_hi_done, u)
                    nc.vector.tensor_tensor(zt_lo[:], zt_ps[:], zt_hi[:].bitcast(F32), ALU.subtract).then_inc(zt_lo_done, 1)
                if a:
                    scores = sc_ps[:, 0:EXPERTS]
                    hold(sc_ready, u + 1)
                    nc.vector.max(best[:, 0:8], scores).then_inc(route_step, 1)
                    dve.wait_ge(route_step, 5 * u + 1)
                    nc.vector.tensor_scalar(best_neg[:], best[:, 0:1], -1.0, None, ALU.mult).then_inc(route_step, 1)
                    nc.vector.match_replace(rest[:], best[:, 0:8], scores, NEG).then_inc(route_step, 1)
                    hold(route_step, 5 * u + 3)
                    nc.vector.max(best[:, 8:16], rest[:]).then_inc(route_step, 1)
                    hold(route_step, 5 * u + 4)
                    nc.vector.match_replace(rest[:], best[:, 8:16], rest[:], NEG).then_inc(route_step, 1)
                    dve.wait_ge(gate_exp, 2 * u + 2)
                    nc.vector.reciprocal(gate_inv[:], gate_sum[:]).then_inc(gate_step, 1)
                    dve.wait_ge(gate_step, 2 * u + 1)
                    dve.wait_ge(route_step, 5 * u + 5)
                    nc.vector.tensor_scalar(gate[:], rest[:], NEG, gate_inv[:], ALU.is_equal, ALU.mult).then_inc(gate_step, 1)
                    dve.wait_ge(gate_step, 2 * u + 2)
                    nc.vector.tensor_tensor(gate[:], gate[:], score_exp[:], ALU.mult).then_inc(gate_ready, 1)
                    dve.wait_ge(gate_ready, u + 1)
                    dve.wait_ge(z_ready, u + 1)
                    if b:
                        dve.wait_ge(zt_ready, u)
                    nc.vector.tensor_tensor(zg[:].rearrange("p (e r) -> p e r", r=RANK),
                                            z_ps[:].rearrange("p (e r) -> p e r", r=RANK),
                                            gate[:].unsqueeze(2).broadcast_to((P, EXPERTS, RANK)), ALU.mult).then_inc(zg_ready, 1)

                def tile_low(q):
                    if f:
                        part = slice(4 * q, 4 * q + 4)
                        low(tp_tile(u + 1, q), xt_lo[:, part, :], xt_hi[:, part, :], tp_ps[q % 2])

                def add_out(q):
                    if b:
                        cols = slice(q * 512, (q + 1) * 512)
                        dve.wait_ge(out_ready, out_place(u - 1, q) + 1)
                        nc.vector.scalar_tensor_tensor(rows[r][:, cols], out_ps[q % 2][:], SCALING, rows[r][:, cols],
                                                       ALU.mult, ALU.add).then_inc(out_taken, 1)

                tile_low(0)
                tile_low(1)
                add_out(0)
                tile_low(2)
                add_out(1)
                tile_low(3)
                add_out(2)
                add_out(3)

            steps(body)(dve)

        @block.scalar
        def _(act):
            def high(n, dst, src):
                act.wait_ge(tp_ready, n + 1)
                nc.scalar.activation(dst, src[:], ACT.Copy).then_inc(tp_hi, 1)

            for h in range(2):
                act.wait_ge(out_ready, h + 1)
                nc.scalar.activation(wqk_hi[:, h * (KD // 2):(h + 1) * (KD // 2), :],
                                     out_ps[h][:].rearrange("p (m e) -> p m e", e=EXPERTS), ACT.Copy).then_inc(wqk_hi_done, 1)
            for s in range(STAGES):
                for q in range(4):
                    high(tp_stage(s, q), part_of_weights((a_hi, b_hi), s, q), tp_ps[q % 2])
            wait_rows(act, 0, STAGES)

            def body(k, r, a, b, f):
                u = RING * k + 1 + r
                if f:
                    t = bass.ds(u + 1, 1)
                    nc.scalar.activation(xn[:], rows[(r + 2) % RING][:], ACT.Identity, bias=shift2[:, t],
                                         scale=rstd2[:, t]).then_inc(xn_ready, 1)
                if b:
                    act.wait_ge(zt_ready, u)
                    act.wait_ge(out_ready, out_place(u - 2, 3) + 1)
                    nc.scalar.activation(zt_hi[:], zt_ps[:], ACT.Copy).then_inc(zt_hi_done, 1)
                if a:
                    act.wait_ge(route_step, 5 * u + 3)
                    if b:
                        act.wait_ge(gate_ready, u)
                    nc.scalar.activation(score_exp[:], sc_ps[:, 0:EXPERTS], ACT.Exp, bias=best_neg[:]).then_inc(gate_exp, 1)
                    act.wait_ge(route_step, 5 * u + 4)
                    nc.scalar.activation(best_exp[:], best[:], ACT.Exp, bias=best_neg[:], accum_out=gate_sum[:]).then_inc(gate_exp, 1)
                if f:
                    for q in range(4):
                        if q == 0 and a:
                            act.wait_ge(z_ready, u + 1)
                        if q == 3 and (u + 2 < TT if isinstance(u, int) else True):
                            wait_rows(act, k, STAGES + 3 + r)
                        high(tp_tile(u + 1, q), xt_hi[:, 4 * q:4 * q + 4, :], tp_ps[q % 2])

            steps(body)(act)


def build_program(nc, x, ctx, a_w, b_w, wq_w, keys, tables, out):
    with ExitStack() as sems, nc.sbuf_tensor("rstd2", [P, TT], F32) as rstd2, nc.sbuf_tensor("shift2", [P, TT], F32) as shift2:
        attention_phase(nc, sems, x, ctx, tables, out, rstd2, shift2)
        ffn_phase(nc, sems, out, a_w, b_w, wq_w, keys, tables, rstd2, shift2, out)


_INS = ["x", "ctx_4096", "L0_ffn_A_w", "L0_ffn_B_w", "L0_ffn_Wq_w", "L0_ffn_keys"]


def kernel(**inputs):
    import numpy as _np
    import concourse.bacc as _bacc
    from concourse import mybir as _mybir
    from concourse.bass_utils import run_bass_kernel_spmd as _run

    nc = _bacc.Bacc("TRN2", target_bir_lowering=False, num_devices=1)
    arrays, args, tabs = {}, [], {}
    for name in _INS:
        a = _np.ascontiguousarray(inputs[name])
        arrays[f"in_{name}_dram"] = a
        args.append(nc.dram_tensor(f"in_{name}_dram", a.shape, _mybir.dt.from_np(a.dtype), kind="ExternalInput").ap())
    for name, a in transform_tables().items():
        arrays[f"table_{name}_dram"] = a
        tabs[name] = nc.dram_tensor(f"table_{name}_dram", a.shape, _mybir.dt.float32, kind="ExternalInput").ap()
    out = nc.dram_tensor("out_0_dram", (B, L, D), _mybir.dt.float32, kind="ExternalOutput").ap()
    build_program(nc, *args, tabs, out)
    r = _run(nc, [arrays], core_ids=[0])
    return r.results[0]["out_0_dram"]
```

```python
from contextlib import ExitStack

import numpy as np

import concourse.bass as bass
from concourse import mybir

F32 = mybir.dt.float32
F32R = mybir.dt.float32r
ALU = mybir.AluOpType
ACT = mybir.ActivationFunctionType

B, L, D = 8, 512, 2048
P = 128
CH = 512
GPB = D // CH
GROUPS = B * GPB
LT = L // P
CT = CH // P
TOPK = 12
NEG = -3.0e38
EPS = 1e-5
NFFN, EXPERTS, RANK, RDIM, TOPE = 512, 64, 8, 16, 16
SCALING = 2.0
TOKENS = B * L
TT = TOKENS // P
KD = D // P
KN = NFFN // P


def transform_tables():
    H = L // 2
    p = np.arange(P)
    cos, sin, pi = np.cos, np.sin, np.pi

    def alt(n):
        return 1.0 - 2.0 * (n % 2)

    cyc = [2 * p, 2 * p + 1]
    neg = [8 * p + 1, 8 * p + 5]
    fwd = []
    for par in range(2):
        for fn in (cos, sin):
            for half in range(2):
                n = p + P * half
                m = fn(2 * pi * np.outer(n + 0.5, cyc[par]) / L)
                if par == 0 and fn is sin:
                    m[:, 0] = alt(n)
                fwd.append(m)
    for par in range(2):
        th = 2 * pi * np.outer(p + 0.5, neg[par]) / (2 * L)
        fwd += [cos(th), sin(th), -sin(th)]
    for half in range(2):
        m = cos(2 * pi * np.outer(p + P * half + 0.5, cyc[0]) / L)
        m[:, 0] = 0.0
        fwd.append(m)
    lags = []
    for par in range(2):
        even = 2.0 * cos(2 * pi * np.outer(cyc[par], np.arange(H + 1)) / L) / L
        if par == 0:
            even[0] = alt(np.arange(H + 1)) / L
        odd = 2.0 * sin(2 * pi * np.outer(cyc[par], np.arange(H)) / L) / L
        odd[:, 0] = 0.0
        if par == 0:
            odd[0] = 0.0
        lags += [even[:, :H] - even[:, H:], odd]
    wts = []
    for par in range(2):
        for fn in (cos, sin):
            for half in range(2):
                f = cyc[par].copy()
                if par == 0:
                    f[0] = H
                m = fn(2 * pi * np.outer(p + P * half, f) / L)
                if fn is cos:
                    m -= 1.0
                    if half == 0:
                        m[0] = alt(f) - 1.0
                elif half == 0:
                    m[0] = 0.0
                if par == 0 and fn is sin:
                    m[:, 0] = 0.0
                wts.append(m)
    for par in range(2):
        for fn in (cos, sin):
            for half in range(2):
                m = fn(2 * pi * np.outer(p + P * half, neg[par]) / (2 * L))
                if half == 0 and fn is sin:
                    m[0] = sin(pi * neg[par] / 2)
                wts.append(m)
    back = []
    for half in range(2):
        t = p + P * half + 0.5
        for par in range(2):
            m = 2.0 * cos(2 * pi * np.outer(cyc[par], t) / L) / (2 * L)
            if par == 0:
                m[0] /= 2
            back.append(m)
        for par in range(2):
            back.append(2.0 * sin(2 * pi * np.outer(neg[par], t) / (2 * L)) / (2 * L))
        for par in range(2):
            m = 2.0 * sin(2 * pi * np.outer(cyc[par], t) / L) / (2 * L)
            if par == 0:
                m[0] = alt(p) / (2 * L)
            back.append(m)
        for par in range(2):
            back.append(2.0 * cos(2 * pi * np.outer(neg[par], t) / (2 * L)) / (2 * L))

    def cat(ms):
        return np.ascontiguousarray(np.concatenate(ms, 1).astype(np.float32))

    return {
        "fwd": cat(fwd), "lags": cat(lags), "wts": cat(wts), "back": cat(back),
        "ident": np.eye(P, dtype=np.float32), "flip": np.ascontiguousarray(np.eye(P, dtype=np.float32)[::-1]),
    }


def attention_phase(nc, sems, x, ctx, tables, x2, rstd2, shift2):
    with ExitStack() as st:
        def sb(name, shape, dt=F32):
            return st.enter_context(nc.sbuf_tensor(name, shape, dt))

        def ps(name, shape):
            return st.enter_context(nc.psum_tensor(name, shape, F32))

        def sem(name):
            return sems.enter_context(nc.semaphore(name))

        fwd = sb("fwd", [P, 16, P])
        wts_hi, wts_lo = sb("wts_hi", [P, 16, P], F32R), sb("wts_lo", [P, 16, P], F32R)
        lags_hi, lags_lo = sb("lags_hi", [P, 2, L], F32R), sb("lags_lo", [P, 2, L], F32R)
        back_hi, back_lo = sb("back_hi", [P, 16, P], F32R), sb("back_lo", [P, 16, P], F32R)
        ident, flip = sb("ident", [P, P]), sb("flip", [P, P])
        stat_in = sb("stat_in", [P, 2, CH])
        bn_x, bn_x2 = sb("bn_x", [P, LT, GPB, 6]), sb("bn_x2", [P, LT, GPB, 6])
        norm_x = [sb(f"norm_x{n}", [P, LT, 2]) for n in range(4)]
        norm_x2 = [sb(f"norm_x2{n}", [P, LT, 2]) for n in range(4)]
        pace, zero = sb("pace", [P, 33]), sb("zero", [P, 1])
        rstd, shift = sb("rstd", [P, B * LT]), sb("shift", [P, B * LT])
        xq = sb("xq", [P, LT, CH])
        q_sum = sb("q_sum", [P, 2, CH])
        v = sb("v", [P, LT, CH])
        v_last, v_last2 = sb("v_last", [P, CH]), sb("v_last2", [P, CH])
        v_fold = sb("v_fold", [P, LT, CH])
        v_cyc = sb("v_cyc", [P, 2, 4, CH])
        v_neg = sb("v_neg", [P, 4, CH])
        prod = sb("prod", [P, 3, 2, CH])
        p_hi, p_lo = sb("p_hi", [P, 4, CH], F32R), sb("p_lo", [P, 4, CH], F32R)
        r_hi, r_lo = sb("r_hi", [P, 8, CH], F32R), sb("r_lo", [P, 8, CH], F32R)
        top = sb("top", [P, CT, 16])
        neg_max, exp_sum, inv_sum = sb("neg_max", [P, CT]), sb("exp_sum", [P, CT]), sb("inv_sum", [P, CT])
        exp_top = sb("exp_top", [P, CT, TOPK])
        e = sb("e", [P, CT, L])
        pick = sb("pick", [P, CT, L])
        w_hi = sb("w_hi", [P, LT, CH], F32R)
        w_lo = [r_hi[:, 2, :], r_hi[:, 3, :], r_lo[:, 2, :], r_lo[:, 3, :]]
        xr = sb("xr", [P, LT, CH])
        rev = sb("rev", [P, 2, CH])

        pair_ps = [[ps(f"pair{s}{n}", [P, CH]) for n in "ab"] for s in range(2)]
        lag_ps = [ps(f"lag{s}", [P, L]) for s in range(2)]
        evac_ps = [ps(f"evac{s}", [P, CH]) for s in range(2)]

        start_loaded, tables_loaded, tables_split = sem("start_loaded"), sem("tables_loaded"), sem("tables_split")
        stat_loaded, stat_used = [sem(f"stat_loaded{n}") for n in range(2)], sem("stat_used")
        x_norm_step, x_sqrt_done, x_norm_ready = sem("x_norm_step"), sem("x_sqrt_done"), sem("x_norm_ready")
        x2_stat, x2_norm_step, x2_sqrt_done, x2_norm_ready = (
            sem("x2_stat"), sem("x2_norm_step"), sem("x2_sqrt_done"), sem("x2_norm_ready"))
        xq_loaded, v_loaded, xr_loaded = sem("xq_loaded"), sem("v_loaded"), sem("xr_loaded")
        normed, q_folded = sem("normed"), sem("q_folded")
        v_folded, v_halves, v_shifted, v_twisted = sem("v_folded"), sem("v_halves"), sem("v_shifted"), sem("v_twisted")
        evac_ready, evac_done, w_lo_done = sem("evac_ready"), sem("evac_done"), sem("w_lo_done")
        pair_ready, pair_done = sem("pair_ready"), sem("pair_done")
        prod_ready, prod_added, sum_ready = sem("prod_ready"), sem("prod_added"), sem("sum_ready")
        hi_done, lo_done = sem("hi_done"), sem("lo_done")
        dc_done = sem("dc_done")
        lag_ready, corr_summed, topk_step, exp_done = sem("lag_ready"), sem("corr_summed"), sem("topk_step"), sem("exp_done")
        odd_copied = sem("odd_copied")
        inv_done, picked, weighted, w_folded = sem("inv_done"), sem("picked"), sem("weighted"), sem("w_folded")
        even_copied, rev_ready, x2_step, flip_used, stored = (
            sem("even_copied"), sem("rev_ready"), sem("x2_step"), sem("flip_used"), sem("stored"))

        x_t = x.rearrange("b (j p) d -> b p j d", p=P)
        ctx_t = ctx.rearrange("b (j p) d -> b p j d", p=P)
        x2_t = x2.rearrange("b (j p) d -> p (b j) d", p=P)

        def quarter(r, off):
            return (2 + r + off) % GPB, (2 + r + off) // GPB

        def at_group(arr, k, r, off):
            q, later = quarter(r, off)
            return arr[bass.ds(k + later, 1), :, :, q * CH:(q + 1) * CH].rearrange("o p j c -> (o p) j c")

        def is_step(i, n):
            return isinstance(i, int) and i == n

        def evac_cyc(i, n):
            return n if is_step(i, 0) else 12 * i - 4 + n

        def evac_wt(i, n):
            return 12 * i + n - (4 if is_step(i, GROUPS) else 0)

        def evac_neg(i, n):
            return 12 * i + 4 + n

        def pair_q(i, n):
            return n if is_step(i, 0) else 8 * i - 6 + n

        def pair_w(i, n):
            return 8 * i - 4 + n - (2 if is_step(i, GROUPS) else 0)

        def pair_o(i, n):
            return 8 * i + n - (2 if is_step(i, GROUPS) else 0)

        def half_p(i, n):
            return n if is_step(i, 0) else 12 * i - 8 + n

        def slot_p(i, n):
            return (n if is_step(i, 0) else n + 1) % 3

        def half_r(i, n):
            return 12 * i - 4 + n - (4 if is_step(i, GROUPS) else 0)

        def slot_r(i, n):
            return (n + 1 if is_step(i, GROUPS) else n + 2) % 3

        def lag_flip(i, n):
            return 6 * i - 4 + n - (4 if is_step(i, GROUPS + 1) else 0)

        def lag_corr(i, n):
            return n if is_step(i, 0) else 6 * i - 2 + n

        def corr_at(i, c, second):
            return 8 * i + 4 * (c // 2) + 2 * second + c % 2 + 1

        def topk_at(i, c, stage):
            return 24 * i + 12 * (c // 2) + 2 * stage + c % 2 + 1

        def exp_at(i, c, small):
            return 8 * i + 4 * (c // 2) + 2 * small + c % 2 + 1

        W_BLOCKS = (2, 3, 0, 1)

        def steps(eng, body):
            body(-1, 2, True, False, False, True)
            body(-1, 3, True, True, False, True)
            with eng.Fori(0, B - 1) as k:
                for r in range(4):
                    body(k, r, True, True, True, True)
            body(B - 1, 0, True, True, True, True)
            body(B - 1, 1, True, True, True, False)
            body(B - 1, 2, False, True, True, False)
            body(B - 1, 3, False, False, True, False)

        def has_stats(k, r):
            return r < 2 and not isinstance(k, int)

        def stat_at(k, r, n):
            return 16 * k + 8 * r + n

        block = st.enter_context(nc.Block())

        @block.sync
        def _(sp):
            def whole(buf):
                return buf[:, 0].rearrange("p j c -> p (j c)") if buf is v_cyc else buf[:].rearrange("p j c -> p (j c)")

            for j, buf in enumerate((pick, e, v_cyc, xr)):
                sp.dma_start(whole(buf), x[0, j * P:(j + 1) * P, :]).then_inc(start_loaded, 16)

            def load_xq(k, r, off):
                sp.dma_start(xq[:], at_group(x_t, k, r, off)).then_inc(xq_loaded, 16)

            def load_v(k, r, off, last_used):
                q, later = quarter(r, off)
                sp.dma_start(v[:], at_group(ctx_t, k, r, off)).then_inc(v_loaded, 16)
                if last_used is not None:
                    sp.wait_ge(dc_done, last_used)
                last = ctx[bass.ds(k + later, 1), L - 1:L, q * CH:(q + 1) * CH].rearrange("o p c -> (o p) c")
                sp.dma_start(v_last[:], last.broadcast_to((P, CH))).then_inc(v_loaded, 16)

            load_v(-1, 2, 0, None)
            load_xq(-1, 2, 0)
            sp.dma_start(fwd[:].rearrange("p n m -> p (n m)"), tables["fwd"]).then_inc(tables_loaded, 16)
            sp.dma_start(ident[:], tables["ident"]).then_inc(tables_loaded, 16)
            sp.dma_start(flip[:], tables["flip"]).then_inc(tables_loaded, 16)
            sp.dma_start(v_neg[:, 0:2, :].rearrange("p n c -> p (n c)"), tables["lags"]).then_inc(tables_loaded, 16)
            sp.dma_start(v_cyc[:, 1].rearrange("p n c -> p (n c)"), tables["wts"]).then_inc(tables_loaded, 16)
            sp.wait_ge(stat_used, 1)
            sp.dma_start(pick[:].rearrange("p n c -> p (n c)"), tables["back"]).then_inc(tables_loaded, 16)

            def body(k, r, a, b, c, f):
                i = 4 * k + 2 + r

                def stat_pair(m):
                    if has_stats(k, r):
                        for h in range(2):
                            n = stat_at(k, r, 2 * m + h)
                            if not (m < 1 and r == 0):
                                sp.wait_ge(stat_used, n)
                            tile, q = (8 * r + 2 * m + h) // GPB, (2 * m + h) % GPB
                            sp.dma_start(stat_in[:, h, :], x[bass.ds(k + 1, 1), tile * P:(tile + 1) * P, q * CH:(q + 1) * CH]
                                         .rearrange("o p c -> (o p) c")).then_inc(stat_loaded[h], 16)

                if has_stats(k, r) and r == 0:
                    sp.wait_ge(x_norm_ready, 2 * (k + 1))
                stat_pair(0)
                if f:
                    sp.wait_ge(pair_ready, pair_q(i, 1) + 1)
                    load_xq(k, r, 1)
                stat_pair(1)
                if f:
                    sp.wait_ge(v_twisted, 2 * i + 2)
                    load_v(k, r, 1, i + 1)
                stat_pair(2)
                stat_pair(3)
                if c:
                    sp.wait_ge(x2_stat, LT * (i - 1))
                    sp.dma_start(x2_t[:, bass.ds(LT * k, LT), r * CH:(r + 1) * CH], xr[:]).then_inc(stored, 16)
                if b:
                    if c:
                        sp.wait_ge(stored, 16 * (i - 1))
                    else:
                        sp.wait_ge(x_norm_ready, 2)
                    sp.dma_start(xr[:], at_group(x_t, k, r, -1)).then_inc(xr_loaded, 16)

            steps(sp, body)
            sp.wait_ge(stored, 16 * GROUPS)

        @block.tensor
        def _(pe):
            def fwd_mm(out, n, rhs, start, stop):
                return nc.tensor.matmul(out[:], fwd[:, n, :], rhs, start=start, stop=stop)

            def split_mm(out, lhs_hi, lhs_lo, rhs_hi, rhs_lo, start, stop):
                nc.tensor.matmul(out, lhs_hi, rhs_hi, start=start, stop=False)
                nc.tensor.matmul(out, lhs_hi, rhs_lo, start=False, stop=False)
                return nc.tensor.matmul(out, lhs_lo, rhs_hi, start=False, stop=stop)

            pe.wait_ge(tables_loaded, 16 * 6)

            def body(k, r, a, b, c, f):
                i = 4 * k + 2 + r
                if a:
                    pe.wait_ge(v_folded, i + 1)
                    for n in range(4):
                        if not (is_step(i, 0) and n < 2):
                            pe.wait_ge(evac_done, evac_cyc(i, n) - 1)
                        bank = evac_ps[n % 2]
                        for h in range(2):
                            last = fwd_mm(bank, 2 * n + h, v_fold[:, 2 * (n // 2) + h, :], h == 0, h == 1)
                        last.then_inc(evac_ready, 1)
                for n in range(2):
                    if a:
                        pe.wait_ge(q_folded, i + 1)
                        if b:
                            pe.wait_ge(pair_done, 2 * (i - 1) + n + 1)
                        bank = pair_ps[n % 2]
                        src = q_sum if n == 0 else xq
                        for h in range(2):
                            fwd_mm(bank[0], 14 + h if n == 0 else 4 + h, src[:, h, :], h == 0, h == 1)
                        for h in range(2):
                            last = fwd_mm(bank[1], 4 * n + 2 + h, src[:, h, :], h == 0, h == 1)
                        last.then_inc(pair_ready, 1)
                    if b:
                        pe.wait_ge(w_folded, 3 * CT * i)
                        for l in (2 * n, 2 * n + 1):
                            if l < 2:
                                pe.wait_ge(evac_done, evac_wt(i, l) - 1)
                            else:
                                pe.wait_ge(w_lo_done, LT * (i - 1) + l - 1)
                            for t in range(CT):
                                last = nc.tensor.transpose(evac_ps[l % 2][:, t * P:(t + 1) * P],
                                                           pick[:, t, l * P:(l + 1) * P], ident[:])
                            last.then_inc(evac_ready, 1)
                if c:
                    for h in range(2):
                        if a or b:
                            pe.wait_ge(corr_summed, corr_at(i - 1, 2 + h, 1))
                        else:
                            pe.wait_ge(flip_used, 2 * (i - 3) + h + 1)
                        pe.wait_ge(rev_ready, 2 * (i - 2) + h + 1)
                        nc.tensor.matmul(lag_ps[h][:], flip[:], rev[:, h, :], start=True, stop=True).then_inc(lag_ready, 1)
                if b:
                    pe.wait_ge(evac_done, evac_wt(i, 3) + 1)
                    pe.wait_ge(w_lo_done, LT * i)
                    for n, blk in enumerate(W_BLOCKS):
                        if n >= 2:
                            pe.wait_ge(prod_ready, half_r(i, 2 * n - 3) + 1)
                        elif a:
                            pe.wait_ge(prod_ready, half_p(i, 2 * n + 1) + 1)
                        else:
                            pe.wait_ge(pair_done, 2 * (i - 1) + n + 1)
                        cos_in, sin_in = (0, 2) if blk < 2 else (2, 0)
                        bank = pair_ps[n % 2]
                        for part, first in enumerate((cos_in, sin_in)):
                            for h in range(2):
                                t = 4 * blk + 2 * part + h
                                last = split_mm(bank[part][:], wts_hi[:, t, :], wts_lo[:, t, :],
                                                w_hi[:, first + h, :], w_lo[first + h], h == 0, h == 1)
                        last.then_inc(pair_ready, 1)
                if a:
                    pe.wait_ge(v_twisted, 2 * i + 2)
                    for n in range(4):
                        if b and n < 2:
                            pe.wait_ge(w_lo_done, LT * (i - 1) + n + 3)
                        else:
                            pe.wait_ge(evac_done, evac_neg(i, n) - 1)
                        bank = evac_ps[n % 2]
                        re, im = (1, 3) if n < 2 else (0, 2)
                        t = 8 + 3 * (n // 2)
                        fwd_mm(bank, t + (n % 2), v_fold[:, re, :], True, False)
                        fwd_mm(bank, t + (2 if n % 2 == 0 else 0), v_fold[:, im, :], False, True).then_inc(evac_ready, 1)

                def corr(tiles):
                    pe.wait_ge(hi_done, half_p(i, 3) + 1)
                    pe.wait_ge(lo_done, half_p(i, 3) + 1)
                    if is_step(i, 0):
                        pe.wait_ge(tables_split, 6)
                    for t in tiles:
                        if t >= 2:
                            pe.wait_ge(corr_summed, corr_at(i, t - 2, 1))
                        elif c:
                            pe.wait_ge(flip_used, 2 * (i - 2) + t + 1)
                        elif b:
                            pe.wait_ge(corr_summed, corr_at(i - 1, 2 + t, 1))
                        ch = slice(t * P, (t + 1) * P)
                        for part, cols in enumerate((slice(0, L // 2), slice(L // 2, L))):
                            for par in range(2):
                                row = 2 * par + part
                                last = split_mm(lag_ps[t % 2][:, cols], p_hi[:, row, ch], p_lo[:, row, ch],
                                                lags_hi[:, par, cols], lags_lo[:, par, cols], par == 0, par == 1)
                        last.then_inc(lag_ready, 1)

                def out(h):
                    pe.wait_ge(hi_done, half_r(i, 7) + 1)
                    pe.wait_ge(lo_done, half_r(i, 7) + 1)
                    pe.wait_ge(prod_ready, half_r(i, 5 + 2 * h) + 1)
                    for part, rows in enumerate(((0, 2, 5, 7), (1, 3, 4, 6))):
                        for n, row in enumerate(rows):
                            t = 8 * h + 4 * part + n
                            last = split_mm(pair_ps[h][part][:], back_hi[:, t, :], back_lo[:, t, :],
                                            r_hi[:, row, :], r_lo[:, row, :], n == 0, n == 3)
                    last.then_inc(pair_ready, 1)

                for h in range(2):
                    if a:
                        corr((2 * h, 2 * h + 1))
                    if b:
                        out(h)

            steps(pe, body)

        @block.vector
        def _(dve):
            held = [0]

            def hold(sem_, value):
                dve.wait_ge(sem_, value)
                nc.vector.memset(pace[:, held[0] % 32:held[0] % 32 + 1], 0.0)
                held[0] += 1

            def norm_begin(bn, tmp, step, n):
                mv, ve = tmp[0], tmp[1]
                for j in range(LT):
                    nc.vector.bn_aggr(mv[:, j, :], bn[:, j, :, :].rearrange("p g s -> p (g s)")).then_inc(step, 1)
                dve.wait_ge(step, 9 * n + 4)
                nc.vector.tensor_scalar(ve[:, :, 0], mv[:, :, 1], EPS, None, ALU.add).then_inc(step, 1)

            def norm_end(tmp, step, sqrt_done, n, scale, shift_, ready):
                mv, ve, sd, t = tmp
                y0, t = sd[:, :, 1], t[:, :, 0]
                cols = bass.ds(LT * n, LT)
                dve.wait_ge(sqrt_done, n + 1)
                nc.vector.reciprocal(y0, sd[:, :, 0]).then_inc(step, 1)
                dve.wait_ge(step, 9 * n + 6)
                nc.vector.tensor_tensor(t, ve[:, :, 0], y0, ALU.mult).then_inc(step, 1)
                dve.wait_ge(step, 9 * n + 7)
                nc.vector.tensor_tensor(t, t, y0, ALU.mult).then_inc(step, 1)
                dve.wait_ge(step, 9 * n + 8)
                nc.vector.tensor_scalar(t, t, -0.5, 1.5, ALU.mult, ALU.add).then_inc(step, 1)
                dve.wait_ge(step, 9 * n + 9)
                nc.vector.tensor_tensor(scale[:, cols], t, y0, ALU.mult).then_inc(ready, 1)
                dve.wait_ge(ready, 2 * n + 1)
                nc.vector.scalar_tensor_tensor(shift_[:, cols], mv[:, :, 0], -1.0, scale[:, cols],
                                               ALU.mult, ALU.mult).then_inc(ready, 1)

            def low_half(n, buf, slot, row):
                dve.wait_ge(hi_done, n + 1)
                nc.vector.tensor_tensor(buf[:, row, :], prod[:, slot, 0, :],
                                        (p_hi if buf is p_lo else r_hi)[:, row, :].bitcast(F32), ALU.subtract).then_inc(lo_done, 1)

            def products(blocks, half, slot_of, pair, spec_of, buf, spec_wait, weights, before_low, between):
                count = 2 * len(blocks)
                for n in range(count):
                    blk = blocks[n // 2]
                    c_ps, s_ps = pair_ps[(n // 2) % 2]
                    c_v, s_v = spec_of(blk)
                    if n % 2 == 0:
                        dve.wait_ge(pair_ready, pair(n // 2) + 1)
                        spec_wait(blk)
                    slot = slot_of(n)
                    if not (isinstance(half(n), int) and half(n) < 3):
                        dve.wait_ge(lo_done, half(n) - 2)
                    first_v, second_v = (c_v, s_v) if n % 2 == 0 else (s_v, c_v)
                    if not weights and n % 2 == 1:
                        nc.vector.tensor_tensor(prod[:, slot, 0, :], s_ps[:], c_v, ALU.mult)
                        op = nc.vector.tensor_tensor(prod[:, slot, 1, :], c_ps[:], s_v, ALU.mult)
                    else:
                        if weights and blk < 2:
                            nc.vector.scalar_tensor_tensor(prod[:, slot, 0, :], c_ps[:], 1.0, first_v, ALU.add, ALU.mult)
                        else:
                            nc.vector.tensor_tensor(prod[:, slot, 0, :], c_ps[:], first_v, ALU.mult)
                        op = nc.vector.tensor_tensor(prod[:, slot, 1, :], s_ps[:], second_v, ALU.mult)
                    op.then_inc(prod_ready, 1)
                    before_low(n)
                    if n >= 2:
                        low_half(half(n - 2), buf, slot_of(n - 2), 2 * blocks[n // 2 - 1] + n % 2)
                    between(n)
                for n in range(count - 2, count):
                    low_half(half(n), buf, slot_of(n), 2 * blocks[n // 2] + n % 2)

            dve.wait_ge(start_loaded, 16 * LT)
            for j, buf in enumerate((pick, e, v_cyc, xr)):
                for q in range(GPB):
                    op = nc.vector.bn_stats(bn_x[:, j, q, :], buf[:, 0, q, :] if buf is v_cyc else buf[:, q, :])
            op.then_inc(stat_used, 1)
            dve.wait_ge(stat_used, 1)
            norm_begin(bn_x, norm_x, x_norm_step, 0)
            norm_end(norm_x, x_norm_step, x_sqrt_done, 0, rstd, shift, x_norm_ready)
            dve.wait_ge(tables_loaded, 16 * 6)
            dve.wait_ge(tables_split, 3)
            nc.vector.tensor_tensor(lags_lo[:], v_neg[:, 0:2, :], lags_hi[:].bitcast(F32), ALU.subtract).then_inc(tables_split, 1)
            for lo, hi, src in ((wts_lo, wts_hi, v_cyc[:, 1]), (back_lo, back_hi, pick)):
                nc.vector.tensor_tensor(lo[:].rearrange("p n m -> p (n m)"), src[:].rearrange("p n c -> p (n c)"),
                                        hi[:].rearrange("p n m -> p (n m)").bitcast(F32), ALU.subtract).then_inc(tables_split, 1)

            def body(k, r, a, b, c, f):
                i = 4 * k + 2 + r
                cyc, cyc_before = r % 2, (r + 1) % 2

                def stat_pair(m):
                    if has_stats(k, r):
                        for h in range(2):
                            tile, q = (8 * r + 2 * m + h) // GPB, (2 * m + h) % GPB
                            dve.wait_ge(stat_loaded[h], 16 * (8 * k + 4 * r + m + 1))
                            nc.vector.bn_stats(bn_x[:, tile, q, :], stat_in[:, h, :]).then_inc(stat_used, 1)

                def weights_low(tiles):
                    for l in tiles:
                        if b:
                            dve.wait_ge(evac_done, evac_wt(i, l) + 1)
                            nc.vector.tensor_tensor(w_lo[l], evac_ps[l % 2][:], w_hi[:, l, :].bitcast(F32),
                                                    ALU.subtract).then_inc(w_lo_done, 1)

                stat_pair(0)
                weights_low((0, 1))
                if not a:
                    weights_low((2, 3))
                if a:
                    products((0, 1), lambda n: half_p(i, n), lambda n: slot_p(i, n), lambda n: pair_q(i, n),
                             lambda blk: (v_cyc[:, cyc, 2 * blk, :], v_cyc[:, cyc, 2 * blk + 1, :]), p_lo,
                             lambda blk: dve.wait_ge(evac_done, evac_cyc(i, 2 * blk + 1) + 1), False,
                             lambda n: weights_low((2, 3)) if n == 2 else None, lambda n: None)
                    dve.wait_ge(prod_ready, half_p(i, 3) + 1)
                    nc.vector.scalar_tensor_tensor(v_cyc[0:1, cyc, 0, :], v_last[0:1, :], float(L), v_cyc[0:1, cyc, 0, :],
                                                   ALU.mult, ALU.add).then_inc(dc_done, 1)
                    if not b:
                        nc.vector.memset(pace[:, 32:33], 0.0).then_inc(pair_done, 2)
                def add_turned():
                    for h in range(2):
                        dve.wait_ge(lag_ready, lag_flip(i, h) + 1)
                        nc.vector.tensor_tensor(xr[:, 3 - h, :], lag_ps[h][:], xr[:, 3 - h, :], ALU.add).then_inc(flip_used, 1)

                def x2_statistics():
                    dve.wait_ge(pair_done, 2 * i)
                    for j in range(LT):
                        if j == 2:
                            dve.wait_ge(flip_used, 2 * (i - 1))
                        nc.vector.bn_stats(bn_x2[:, j, r, :], xr[:, j, :]).then_inc(x2_stat, 1)
                    if r == 3:
                        hold(x2_stat, LT * (i - 1))
                        norm_begin(bn_x2, norm_x2, x2_norm_step, k)

                if c and not b:
                    add_turned()
                if b:
                    dve.wait_ge(dc_done, i)

                    def spec_wait(blk):
                        if blk >= 2:
                            dve.wait_ge(evac_done, evac_neg(i - 1, 2 * (blk - 2) + 1) + 1)

                    def between(n):
                        if n == 3:
                            if c:
                                add_turned()
                            stat_pair(1)
                        if n == 5:
                            stat_pair(2)

                    products(W_BLOCKS, lambda n: half_r(i, n), lambda n: slot_r(i, n), lambda n: pair_w(i, n),
                             lambda blk: ((v_cyc[:, cyc_before, 2 * blk, :], v_cyc[:, cyc_before, 2 * blk + 1, :]) if blk < 2
                                          else (v_neg[:, 2 * blk - 4, :], v_neg[:, 2 * blk - 3, :])), r_lo,
                             spec_wait, True, lambda n: None, between)
                stat_pair(3)
                if has_stats(k, r) and r == 1:
                    hold(stat_used, 16 * k + 17)
                    norm_begin(bn_x, norm_x, x_norm_step, k + 1)
                if c:
                    x2_statistics()
                if has_stats(k, r) and r == 1:
                    norm_end(norm_x, x_norm_step, x_sqrt_done, k + 1, rstd, shift, x_norm_ready)
                if a:
                    def sums(t, second):
                        even, odd = lag_ps[t % 2][:, 0:L // 2], e[:, t, L // 2:L]
                        if not second:
                            dve.wait_ge(odd_copied, CT * i + t + 1)
                            op = nc.vector.tensor_tensor(e[:, t, 0:L // 2], even, odd, ALU.add)
                        else:
                            dve.wait_ge(corr_summed, corr_at(i, t, 0))
                            op = nc.vector.tensor_tensor(odd[:, 1:], even[:, 1:], odd[:, 1:], ALU.subtract)
                        op.then_inc(corr_summed, 1)

                    def topk(t, stage):
                        if stage == 0:
                            hold(corr_summed, corr_at(i, t, 1))
                            op = nc.vector.max(top[:, t, 0:8], e[:, t, :])
                        elif stage == 1:
                            dve.wait_ge(topk_step, topk_at(i, t, 0))
                            op = nc.vector.tensor_scalar(neg_max[:, t:t + 1], top[:, t, 0:1], -1.0, None, ALU.mult)
                        elif stage == 2:
                            op = nc.vector.match_replace(pick[:, t, :], top[:, t, 0:8], e[:, t, :], NEG)
                        elif stage == 3:
                            hold(topk_step, topk_at(i, t, 2))
                            op = nc.vector.max(top[:, t, 8:16], pick[:, t, :])
                        elif stage == 4:
                            dve.wait_ge(topk_step, topk_at(i, t, 3))
                            op = nc.vector.memset(top[:, t, TOPK:16], NEG)
                        else:
                            hold(topk_step, topk_at(i, t, 4))
                            op = nc.vector.match_replace(pick[:, t, :], top[:, t, 8:16], pick[:, t, :], NEG)
                        op.then_inc(topk_step, 1)

                    def choose(t):
                        dve.wait_ge(exp_done, exp_at(i, t, True))
                        nc.vector.reciprocal(inv_sum[:, t:t + 1], exp_sum[:, t:t + 1]).then_inc(inv_done, 1)
                        dve.wait_ge(topk_step, topk_at(i, t, 5))
                        nc.vector.scalar_tensor_tensor(e[:, t, :], pick[:, t, :], NEG, e[:, t, :],
                                                       ALU.is_equal, ALU.mult).then_inc(picked, 1)

                    for pair in ((0, 1), (2, 3)):
                        for second in (0, 1):
                            for t in pair:
                                sums(t, second)
                        for stage in range(6):
                            for t in pair:
                                topk(t, stage)
                            if pair[0] and stage == 2:
                                choose(0)
                                choose(1)
                    choose(2)
                    choose(3)
                if b:
                    dve.wait_ge(xr_loaded, 16 * i)
                    for h in range(2):
                        n = 2 * (i - 1) + h
                        even, odd = pair_ps[h]
                        dve.wait_ge(even_copied, n + 1)
                        nc.vector.tensor_tensor(xr[:, h, :], even[:], xr[:, h, :], ALU.add).then_inc(x2_step, 1)
                        nc.vector.tensor_tensor(rev[:, h, :], rev[:, h, :], odd[:], ALU.subtract).then_inc(rev_ready, 1)
                        dve.wait_ge(x2_step, n + 1)
                        nc.vector.tensor_tensor(xr[:, h, :], odd[:], xr[:, h, :], ALU.add).then_inc(pair_done, 1)
                if c and r == 3:
                    norm_end(norm_x2, x2_norm_step, x2_sqrt_done, k, rstd2, shift2, x2_norm_ready)

            steps(dve, body)

        @block.scalar
        def _(act):
            def norm_inputs(k, r, off):
                act.wait_ge(xq_loaded, 16 * (4 * k + 2 + r + off) + 16)
                act.wait_ge(x_norm_ready, 2 * (k + quarter(r, off)[1]) + 2)

            def norm(k, r, off, tiles):
                batch = k + quarter(r, off)[1]
                for j in tiles:
                    t = bass.ds(LT * batch + j, 1)
                    nc.scalar.activation(xq[:, j, :], xq[:, j, :], ACT.Identity, bias=shift[:, t], scale=rstd[:, t]).then_inc(normed, 1)

            def halves(i):
                act.wait_ge(v_folded, i + 1)
                for tile, src in ((1, 3), (3, 1)):
                    nc.scalar.activation(v[:, tile, :], v_fold[:, src, :], ACT.Copy, scale=0.5 ** 0.5).then_inc(v_halves, 1)
                nc.scalar.activation(v_last2[:], v_last[:], ACT.Copy, scale=2.0 ** 0.5).then_inc(v_halves, 1)

            def weigh(i, t):
                act.wait_ge(inv_done, CT * i + t + 1)
                act.wait_ge(picked, CT * i + t + 1)
                nc.scalar.activation(e[:, t, :], e[:, t, :], ACT.Copy, scale=inv_sum[:, t:t + 1]).then_inc(weighted, 1)

            def high_half(n, buf, slot, row):
                act.wait_ge(sum_ready, n + 1)
                nc.scalar.activation(buf[:, row, :], prod[:, slot, 0, :], ACT.Copy).then_inc(hi_done, 1)

            def evac(n, dst, src):
                act.wait_ge(evac_ready, n + 1)
                nc.scalar.activation(dst, src[:], ACT.Copy).then_inc(evac_done, 1)

            def sqrt(tmp, step, done, n):
                act.wait_ge(step, 9 * n + 5)
                nc.scalar.activation(tmp[2][:, :, 0], tmp[1][:, :, 0], ACT.Sqrt).then_inc(done, 1)

            sqrt(norm_x, x_norm_step, x_sqrt_done, 0)
            norm_inputs(-1, 2, 0)
            norm(-1, 2, 0, range(LT))
            halves(0)
            act.wait_ge(tables_loaded, 16 * 6)
            nc.scalar.activation(lags_hi[:], v_neg[:, 0:2, :], ACT.Copy).then_inc(tables_split, 1)
            for hi, src in ((wts_hi, v_cyc[:, 1]), (back_hi, pick)):
                nc.scalar.activation(hi[:].rearrange("p n m -> p (n m)"), src[:].rearrange("p n c -> p (n c)"),
                                     ACT.Copy).then_inc(tables_split, 1)

            def body(k, r, a, b, c, f):
                i = 4 * k + 2 + r
                if a:
                    if b:
                        act.wait_ge(prod_ready, half_p(i, 0))
                    else:
                        act.wait_ge(tables_split, 6)
                    for n in (0, 1):
                        evac(evac_cyc(i, n), v_cyc[:, r % 2, n, :], evac_ps[n % 2])
                if b:
                    for t in (2, 3):
                        weigh(i - 1, t)
                if a:
                    for n in (2, 3):
                        evac(evac_cyc(i, n), v_cyc[:, r % 2, n, :], evac_ps[n % 2])
                if b:
                    for l in range(LT):
                        evac(evac_wt(i, l), w_hi[:, l, :], evac_ps[l % 2])
                if a:
                    for n in range(4):
                        high_half(half_p(i, n), p_hi, slot_p(i, n), n)
                if b:
                    if c:
                        act.wait_ge(pair_ready, pair_o(i - 1, 1) + 1)
                for n in range(12):
                    if b and n in (0, 1, 2, 3, 4, 5, 7, 9):
                        m = n if n < 6 else (n + 5) // 2
                        high_half(half_r(i, m), r_hi, slot_r(i, m), 2 * W_BLOCKS[m // 2] + m % 2)
                    elif a and n in (6, 8, 10, 11):
                        m = (n - 6) // 2 if n < 11 else 3
                        if b:
                            act.wait_ge(prod_ready, half_r(i, 2 * (m // 2) + 1) + 1)
                        if m == 3 and f and not (has_stats(k, r) and r == 1):
                            norm_inputs(k, r, 1)
                        evac(evac_neg(i, m), v_neg[:, m, :], evac_ps[m % 2])

                def odd_copies(tiles):
                    for t in tiles:
                        act.wait_ge(lag_ready, lag_corr(i, t) + 1)
                        nc.scalar.activation(e[:, t, L // 2:L], lag_ps[t % 2][:, L // 2:L], ACT.Copy).then_inc(odd_copied, 1)

                if has_stats(k, r) and r == 1:
                    sqrt(norm_x, x_norm_step, x_sqrt_done, k + 1)
                if a:
                    odd_copies((0,))
                    if has_stats(k, r) and r == 1:
                        norm_inputs(k, r, 1)
                    odd_copies((1,))
                if f:
                    norm(k, r, 1, range(LT))
                    halves(i + 1)
                if c and r == 3:
                    sqrt(norm_x2, x2_norm_step, x2_sqrt_done, k)
                if a:
                    odd_copies((2, 3))

                def big_exp(t):
                    act.wait_ge(topk_step, topk_at(i, t, 2))
                    nc.scalar.activation(e[:, t, :], e[:, t, :], ACT.Exp, bias=neg_max[:, t:t + 1]).then_inc(exp_done, 1)

                def top_exp(t):
                    act.wait_ge(topk_step, topk_at(i, t, 3))
                    nc.scalar.activation(exp_top[:, t, :], top[:, t, 0:TOPK], ACT.Exp, bias=neg_max[:, t:t + 1],
                                         accum_out=exp_sum[:, t:t + 1]).then_inc(exp_done, 1)

                if a:
                    for t in (0, 1):
                        big_exp(t)
                    for t in (0, 1):
                        top_exp(t)
                    for t in (2, 3):
                        big_exp(t)
                    for t in (0, 1):
                        weigh(i, t)
                    for t in (2, 3):
                        top_exp(t)
                if b:
                    for h in range(2):
                        act.wait_ge(pair_ready, pair_o(i, h) + 1)
                        nc.scalar.activation(rev[:, h, :], pair_ps[h][0][:], ACT.Copy).then_inc(even_copied, 1)
            steps(act, body)

        @block.gpsimd
        def _(pool):
            def fold_v(g):
                pool.wait_ge(v_loaded, 32 * g + 32)
                nc.gpsimd.tensor_tensor(v_fold[:, 0:2, :], v[:, 0:2, :], v[:, 2:4, :], ALU.add)
                nc.gpsimd.tensor_tensor(v_fold[:, 2:4, :], v[:, 0:2, :], v[:, 2:4, :], ALU.subtract).then_inc(v_folded, 1)

            def fold_q(g):
                pool.wait_ge(normed, LT * g + LT)
                nc.gpsimd.tensor_tensor(q_sum[:], xq[:, 0:2, :], xq[:, 2:4, :], ALU.add)
                nc.gpsimd.tensor_tensor(xq[:, 0:2, :], xq[:, 0:2, :], xq[:, 2:4, :], ALU.subtract).then_inc(q_folded, 1)

            def shift_v(g):
                pool.wait_ge(v_folded, g + 1)
                last = v_last[:].unsqueeze(1).broadcast_to((P, 2, CH))
                nc.gpsimd.tensor_tensor(v[:, 0:4:2, :], v[:, 0:4:2, :], last, ALU.subtract).then_inc(v_shifted, 1)
                pool.wait_ge(v_halves, 3 * g + 3)
                nc.gpsimd.tensor_tensor(v[:, 3, :], v[:, 3, :], v_last2[:], ALU.subtract).then_inc(v_shifted, 1)

            def twist_v(i):
                pool.wait_ge(v_shifted, 2 * i + 2)
                pool.wait_ge(evac_ready, evac_cyc(i, 3) + 1)
                nc.gpsimd.tensor_tensor(v_fold[:, 1:4:2, :], v[:, 0:4:2, :], v[:, 1:4:2, :], ALU.add).then_inc(v_twisted, 1)
                nc.gpsimd.tensor_tensor(v_fold[:, 0:4:2, :], v[:, 0:4:2, :], v[:, 1:4:2, :], ALU.subtract).then_inc(v_twisted, 1)

            def add_half(n, slot, op, dc_row, dc):
                pool.wait_ge(prod_ready, n + 1)
                ins = nc.gpsimd.tensor_tensor(prod[:, slot, 0, :], prod[:, slot, 0, :], prod[:, slot, 1, :], op)
                if dc_row is not None:
                    ins.then_inc(prod_added, 1)
                    pool.wait_ge(prod_added, dc)
                    ins = nc.gpsimd.tensor_tensor(prod[0:1, slot, 0, :], dc_row, zero[0:1, :].broadcast_to((1, CH)), ALU.add)
                ins.then_inc(sum_ready, 1)

            def fold_w(i, t):
                pool.wait_ge(weighted, CT * i + t + 1)
                up, down = e[:, t, 1:L // 2], e[:, t, L // 2 + 1:L]
                nc.gpsimd.tensor_tensor(pick[:, t, 1:L // 2], up, down, ALU.add).then_inc(w_folded, 1)
                nc.gpsimd.tensor_tensor(pick[:, t, L // 2 + 1:L], up, down, ALU.subtract).then_inc(w_folded, 1)
                nc.gpsimd.tensor_copy(pick[:, t, 0:L:L // 2], e[:, t, L // 2::-(L // 2)]).then_inc(w_folded, 1)

            nc.gpsimd.memset(zero[:], 0.0).then_inc(prod_added, 1)
            fold_v(0)
            shift_v(0)
            fold_q(0)

            def body(k, r, a, b, c, f):
                i = 4 * k + 2 + r
                if b:
                    for t in range(CT):
                        fold_w(i - 1, t)
                if a:
                    twist_v(i)
                    for n in range(4):
                        add_half(half_p(i, n), slot_p(i, n), ALU.add if n % 2 == 0 else ALU.subtract, None, None)
                if b:
                    for n in range(8):
                        blk = W_BLOCKS[n // 2]
                        dc_row = v_cyc[0:1, (r + 1) % 2, 0, :] if blk == 0 and n % 2 == 0 else None
                        add_half(half_r(i, n), slot_r(i, n), ALU.add if n % 2 == 0 else ALU.subtract, dc_row, i + 1)
                if f:
                    pool.wait_ge(evac_ready, evac_neg(i, 3) + 1)
                    fold_v(i + 1)
                    shift_v(i + 1)
                    fold_q(i + 1)

            steps(pool, body)


def ffn_phase(nc, sems, x2, a_w, b_w, wq_w, keys, tables, rstd2, shift2, out):
    with ExitStack() as st:
        def sb(name, shape, dt=F32):
            return st.enter_context(nc.sbuf_tensor(name, shape, dt))

        def ps(name, shape):
            return st.enter_context(nc.psum_tensor(name, shape, F32))

        def sem(name):
            return sems.enter_context(nc.semaphore(name))

        RING = 4
        a_hi, a_lo = sb("a_hi", [P, KD, NFFN], F32R), sb("a_lo", [P, KD, NFFN], F32R)
        b_hi, b_lo = sb("b_hi", [P, KN, D], F32R), sb("b_lo", [P, KN, D], F32R)
        wqk = sb("wqk", [P, KD, 2, EXPERTS], F32R)
        ident2, keys_sb, keys_t = sb("ident2", [P, P]), sb("keys_sb", [EXPERTS, RDIM]), sb("keys_t", [RDIM, EXPERTS])
        rows = [sb(f"rows{n}", [P, D]) for n in range(RING)]
        xn = sb("xn", [P, D])
        xt_hi, xt_lo = sb("xt_hi", [P, KD, P], F32R), sb("xt_lo", [P, KD, P], F32R)
        zg = sb("zg", [P, NFFN])
        zt_hi, zt_lo = sb("zt_hi", [P, KN, P], F32R), sb("zt_lo", [P, KN, P], F32R)
        best, best_neg, best_exp = sb("best", [P, TOPE]), sb("best_neg", [P, 1]), sb("best_exp", [P, TOPE])
        gate_sum, gate_inv = sb("gate_sum", [P, 1]), sb("gate_inv", [P, 1])
        scores, scores_lo = sb("scores", [P, EXPERTS]), sb("scores_lo", [P, EXPERTS])
        rest, score_exp, gate = sb("rest", [P, EXPERTS]), sb("score_exp", [P, EXPERTS]), sb("gate", [P, EXPERTS])
        pace2 = sb("pace2", [P, 32])

        tp_ps = [ps(f"tp{n}", [P, 4, P]) for n in range(2)]
        z_ps, sc_ps, zt_ps = ps("z", [P, NFFN]), ps("score_sums", [P, NFFN]), ps("zt", [P, KN, P])
        out_ps = [ps(f"out{n}", [P, 512]) for n in range(2)]

        small_loaded, out_stored = sem("small_loaded"), sem("out_stored")
        rows_loaded = [sem(f"rows_loaded{n}") for n in range(RING)]
        keys_turned, keys_copied, wqk_hi_done = sem("keys_turned"), sem("keys_copied"), sem("wqk_hi_done")
        xn_ready, tp_ready, tp_hi, tp_lo = sem("xn_ready"), sem("tp_ready"), sem("tp_hi"), sem("tp_lo")
        sc_ready, sc_summed, route_step, gate_exp = sem("sc_ready"), sem("sc_summed"), sem("route_step"), sem("gate_exp")
        gate_step, gate_ready = sem("gate_step"), sem("gate_ready")
        z_ready, zg_ready, zt_ready, zt_hi_done, zt_lo_done = (
            sem("z_ready"), sem("zg_ready"), sem("zt_ready"), sem("zt_hi_done"), sem("zt_lo_done"))
        out_ready, out_taken = sem("out_ready"), sem("out_taken")

        STAGES = 2 * KN
        x2_rows = x2.rearrange("b l d -> (b l) d").rearrange("(t p) d -> t p d", p=P)
        out_rows = out.rearrange("b l d -> (b l) d").rearrange("(t p) d -> t p d", p=P)
        b_rows = b_w.rearrange("(s t p) n -> s p t n", p=P, t=KN)

        def part_of_weights(w, s, q):
            a_t, b_t = w
            if s < KN:
                return a_t[:, 4 * q:4 * q + 4, s * P:(s + 1) * P]
            col = (4 * (s - KN) + q) * P
            return b_t[:, :, col:col + P]

        def tp_stage(s, q):
            return 4 * s + q

        def tp_tile(t, q):
            return 4 * (STAGES + t) + q

        def wait_rows(eng, k, n):
            eng.wait_ge(rows_loaded[n % RING], 16 * (k + n // RING + 1))

        def out_place(t, q):
            return 2 + 4 * t + q

        def steps(body):
            def run(eng):
                body(-1, 2, False, False, True)
                body(-1, 3, True, False, True)
                with eng.Fori(0, TT // RING - 1) as k:
                    for r in range(RING):
                        body(k, r, True, True, True)
                for r in range(RING):
                    body(TT // RING - 1, r, r < 3, True, r < 2)
            return run

        block = st.enter_context(nc.Block())

        @block.sync
        def _(sp):
            sp.dma_start(ident2[:], tables["ident"]).then_inc(small_loaded, 16)
            sp.dma_start(keys_sb[:], keys).then_inc(small_loaded, 16)
            for s in range(STAGES + RING):
                if s >= RING:
                    sp.wait_ge(tp_ready, tp_stage(s - RING, 3) + 1)
                buf = rows[s % RING]
                if s < KN:
                    sp.dma_start(buf[:], a_w[s * P:(s + 1) * P, :]).then_inc(rows_loaded[s % RING], 16)
                elif s < STAGES:
                    sp.dma_start(buf[:].rearrange("p (t n) -> p t n", t=KN), b_rows[s - KN]).then_inc(rows_loaded[s % RING], 16)
                else:
                    sp.dma_start(buf[:], x2_rows[s - STAGES]).then_inc(rows_loaded[s % RING], 16)
                if s == 0:
                    sp.dma_start(xn[0:RDIM, :], wq_w).then_inc(small_loaded, 16)

            def body(k, r, a, b, f):
                u = RING * k + 1 + r
                if b:
                    sp.wait_ge(out_taken, out_place(u - 1, 3) + 1)
                    sp.dma_start(out_rows[bass.ds(u - 1, 1)].rearrange("o p d -> (o p) d"), rows[r][:]).then_inc(out_stored, 16)
                if b and not isinstance(k, int):
                    sp.wait_ge(out_stored, 16 * u)
                    sp.dma_start(rows[r][:], x2_rows[bass.ds(u + 3, 1)].rearrange("o p d -> (o p) d")).then_inc(rows_loaded[r], 16)

            steps(body)(sp)
            sp.wait_ge(out_stored, 16 * TT)

        @block.tensor
        def _(pe):
            def split_mm(dst, lhs_hi, lhs_lo, rhs_hi, rhs_lo, start, stop):
                nc.tensor.matmul(dst, lhs_hi, rhs_hi, start=start, stop=False)
                nc.tensor.matmul(dst, lhs_hi, rhs_lo, start=False, stop=False)
                return nc.tensor.matmul(dst, lhs_lo, rhs_hi, start=False, stop=stop)

            def transposes(n, q, src):
                if not (isinstance(n, int) and n < 2):
                    pe.wait_ge(tp_lo, n - 1)
                for m in range(4):
                    last = nc.tensor.transpose(tp_ps[q % 2][:, m, :], src[:, (4 * q + m) * P:(4 * q + m + 1) * P], ident2[:])
                last.then_inc(tp_ready, 1)

            pe.wait_ge(small_loaded, 16 * 3)
            nc.tensor.transpose(zt_ps[0:RDIM, 0, 0:EXPERTS], keys_sb[:], ident2[0:EXPERTS, 0:EXPERTS]).then_inc(keys_turned, 1)
            pe.wait_ge(keys_copied, 1)
            for h in range(2):
                for m in range(KD // 2):
                    kt = h * (KD // 2) + m
                    last = nc.tensor.matmul(out_ps[h][:, m * EXPERTS:(m + 1) * EXPERTS], xn[0:RDIM, kt * P:(kt + 1) * P],
                                            keys_t[:], start=True, stop=True)
                last.then_inc(out_ready, 1)
            for s in range(STAGES):
                wait_rows(pe, 0, s)
                for q in range(4):
                    transposes(tp_stage(s, q), q, rows[s % RING])

            def body(k, r, a, b, f):
                u = RING * k + 1 + r
                if a:
                    pe.wait_ge(tp_hi, tp_tile(u, 3) + 1)
                    pe.wait_ge(tp_lo, tp_tile(u, 3) + 1)
                    if b:
                        pe.wait_ge(sc_summed, 2 * u)
                    else:
                        pe.wait_ge(wqk_hi_done, 2)
                        pe.wait_ge(out_taken, 2)
                    for kt in range(KD):
                        nc.tensor.matmul(sc_ps[:, 0:2 * EXPERTS], xt_hi[:, kt, :], wqk[:, kt, :, :].rearrange("p s e -> p (s e)"),
                                         start=kt == 0, stop=False)
                        last = nc.tensor.matmul(sc_ps[:, 0:EXPERTS], xt_lo[:, kt, :], wqk[:, kt, 0, :],
                                                start=False, stop=kt == KD - 1)
                    last.then_inc(sc_ready, 1)
                if b:
                    pe.wait_ge(zg_ready, u)
                    for m in range(KN):
                        last = nc.tensor.transpose(zt_ps[:, m, :], zg[:, m * P:(m + 1) * P], ident2[:])
                    last.then_inc(zt_ready, 1)
                if a:
                    for kt in range(KD):
                        last = split_mm(z_ps[:], xt_hi[:, kt, :], xt_lo[:, kt, :], a_hi[:, kt, :], a_lo[:, kt, :],
                                        kt == 0, kt == KD - 1)
                    last.then_inc(z_ready, 1)

                def tile_transposes(q):
                    if f:
                        if q == 0:
                            pe.wait_ge(xn_ready, u + 2)
                        transposes(tp_tile(u + 1, q), q, xn)

                def out_bank(q):
                    if b:
                        pe.wait_ge(out_taken, out_place(u - 1, q) - 1)
                        for m in range(KN):
                            cols = slice(q * 512, (q + 1) * 512)
                            last = split_mm(out_ps[q % 2][:], zt_hi[:, m, :], zt_lo[:, m, :],
                                            b_hi[:, m, cols], b_lo[:, m, cols], m == 0, m == KN - 1)
                        last.then_inc(out_ready, 1)

                tile_transposes(0)
                tile_transposes(1)
                if b:
                    pe.wait_ge(zt_hi_done, u)
                    pe.wait_ge(zt_lo_done, u)
                out_bank(0)
                tile_transposes(2)
                out_bank(1)
                tile_transposes(3)
                out_bank(2)
                out_bank(3)

            steps(body)(pe)

        @block.vector
        def _(dve):
            held = [0]

            def hold(sem_, value):
                dve.wait_ge(sem_, value)
                nc.vector.memset(pace2[:, held[0] % 32:held[0] % 32 + 1], 0.0)
                held[0] += 1

            def low(n, dst, hi, src):
                dve.wait_ge(tp_hi, n + 1)
                nc.vector.tensor_tensor(dst, src[:], hi.bitcast(F32), ALU.subtract).then_inc(tp_lo, 1)

            dve.wait_ge(keys_turned, 1)
            nc.vector.tensor_copy(keys_t[:], zt_ps[0:RDIM, 0, 0:EXPERTS]).then_inc(keys_copied, 1)
            for h in range(2):
                dve.wait_ge(wqk_hi_done, h + 1)
                part = slice(h * (KD // 2), (h + 1) * (KD // 2))
                nc.vector.tensor_tensor(wqk[:, part, 1, :], out_ps[h][:].rearrange("p (m e) -> p m e", e=EXPERTS),
                                        wqk[:, part, 0, :].bitcast(F32), ALU.subtract).then_inc(out_taken, 1)
            for s in range(STAGES):
                for q in range(4):
                    hi, lo = (part_of_weights(w, s, q) for w in ((a_hi, b_hi), (a_lo, b_lo)))
                    low(tp_stage(s, q), lo, hi, tp_ps[q % 2])

            def body(k, r, a, b, f):
                u = RING * k + 1 + r
                if b:
                    dve.wait_ge(zt_hi_done, u)
                    nc.vector.tensor_tensor(zt_lo[:], zt_ps[:], zt_hi[:].bitcast(F32), ALU.subtract).then_inc(zt_lo_done, 1)
                if a:
                    dve.wait_ge(sc_ready, u + 1)
                    nc.vector.tensor_copy(scores_lo[:], sc_ps[:, EXPERTS:2 * EXPERTS]).then_inc(sc_summed, 1)
                    dve.wait_ge(sc_summed, 2 * u + 1)
                    nc.vector.tensor_tensor(scores[:], sc_ps[:, 0:EXPERTS], scores_lo[:], ALU.add).then_inc(sc_summed, 1)
                    hold(sc_summed, 2 * u + 2)
                    nc.vector.max(best[:, 0:8], scores[:]).then_inc(route_step, 1)
                    dve.wait_ge(route_step, 5 * u + 1)
                    nc.vector.tensor_scalar(best_neg[:], best[:, 0:1], -1.0, None, ALU.mult).then_inc(route_step, 1)
                    nc.vector.match_replace(rest[:], best[:, 0:8], scores[:], NEG).then_inc(route_step, 1)
                    hold(route_step, 5 * u + 3)
                    nc.vector.max(best[:, 8:16], rest[:]).then_inc(route_step, 1)
                    hold(route_step, 5 * u + 4)
                    nc.vector.match_replace(rest[:], best[:, 8:16], rest[:], NEG).then_inc(route_step, 1)
                    dve.wait_ge(gate_exp, 2 * u + 2)
                    nc.vector.reciprocal(gate_inv[:], gate_sum[:]).then_inc(gate_step, 1)
                    dve.wait_ge(gate_step, 2 * u + 1)
                    dve.wait_ge(route_step, 5 * u + 5)
                    nc.vector.tensor_scalar(gate[:], rest[:], NEG, gate_inv[:], ALU.is_equal, ALU.mult).then_inc(gate_step, 1)
                    dve.wait_ge(gate_step, 2 * u + 2)
                    nc.vector.tensor_tensor(gate[:], gate[:], score_exp[:], ALU.mult).then_inc(gate_ready, 1)
                    dve.wait_ge(gate_ready, u + 1)
                    dve.wait_ge(z_ready, u + 1)
                    if b:
                        dve.wait_ge(zt_ready, u)
                    nc.vector.tensor_tensor(zg[:].rearrange("p (e r) -> p e r", r=RANK),
                                            z_ps[:].rearrange("p (e r) -> p e r", r=RANK),
                                            gate[:].unsqueeze(2).broadcast_to((P, EXPERTS, RANK)), ALU.mult).then_inc(zg_ready, 1)

                def tile_low(q):
                    if f:
                        part = slice(4 * q, 4 * q + 4)
                        low(tp_tile(u + 1, q), xt_lo[:, part, :], xt_hi[:, part, :], tp_ps[q % 2])

                def add_out(q):
                    if b:
                        cols = slice(q * 512, (q + 1) * 512)
                        dve.wait_ge(out_ready, out_place(u - 1, q) + 1)
                        nc.vector.scalar_tensor_tensor(rows[r][:, cols], out_ps[q % 2][:], SCALING, rows[r][:, cols],
                                                       ALU.mult, ALU.add).then_inc(out_taken, 1)

                tile_low(0)
                tile_low(1)
                add_out(0)
                tile_low(2)
                add_out(1)
                tile_low(3)
                add_out(2)
                add_out(3)

            steps(body)(dve)

        @block.scalar
        def _(act):
            def high(n, dst, src):
                act.wait_ge(tp_ready, n + 1)
                nc.scalar.activation(dst, src[:], ACT.Copy).then_inc(tp_hi, 1)

            for h in range(2):
                act.wait_ge(out_ready, h + 1)
                nc.scalar.activation(wqk[:, h * (KD // 2):(h + 1) * (KD // 2), 0, :],
                                     out_ps[h][:].rearrange("p (m e) -> p m e", e=EXPERTS), ACT.Copy).then_inc(wqk_hi_done, 1)
            for s in range(STAGES):
                for q in range(4):
                    high(tp_stage(s, q), part_of_weights((a_hi, b_hi), s, q), tp_ps[q % 2])
            wait_rows(act, 0, STAGES)

            def body(k, r, a, b, f):
                u = RING * k + 1 + r
                if f:
                    t = bass.ds(u + 1, 1)
                    nc.scalar.activation(xn[:], rows[(r + 2) % RING][:], ACT.Identity, bias=shift2[:, t],
                                         scale=rstd2[:, t]).then_inc(xn_ready, 1)
                if b:
                    act.wait_ge(zt_ready, u)
                    act.wait_ge(out_ready, out_place(u - 2, 3) + 1)
                    nc.scalar.activation(zt_hi[:], zt_ps[:], ACT.Copy).then_inc(zt_hi_done, 1)
                if a:
                    act.wait_ge(route_step, 5 * u + 3)
                    if b:
                        act.wait_ge(gate_ready, u)
                    nc.scalar.activation(score_exp[:], scores[:], ACT.Exp, bias=best_neg[:]).then_inc(gate_exp, 1)
                    act.wait_ge(route_step, 5 * u + 4)
                    nc.scalar.activation(best_exp[:], best[:], ACT.Exp, bias=best_neg[:], accum_out=gate_sum[:]).then_inc(gate_exp, 1)
                if f:
                    for q in range(4):
                        if q == 0 and a:
                            act.wait_ge(z_ready, u + 1)
                        if q == 3 and (u + 2 < TT if isinstance(u, int) else True):
                            wait_rows(act, k, STAGES + 3 + r)
                        high(tp_tile(u + 1, q), xt_hi[:, 4 * q:4 * q + 4, :], tp_ps[q % 2])

            steps(body)(act)


def build_program(nc, x, ctx, a_w, b_w, wq_w, keys, tables, out):
    with ExitStack() as sems, nc.sbuf_tensor("rstd2", [P, TT], F32) as rstd2, nc.sbuf_tensor("shift2", [P, TT], F32) as shift2:
        attention_phase(nc, sems, x, ctx, tables, out, rstd2, shift2)
        ffn_phase(nc, sems, out, a_w, b_w, wq_w, keys, tables, rstd2, shift2, out)


_INS = ["x", "ctx_4096", "L0_ffn_A_w", "L0_ffn_B_w", "L0_ffn_Wq_w", "L0_ffn_keys"]


def kernel(**inputs):
    import numpy as _np
    import concourse.bacc as _bacc
    from concourse import mybir as _mybir
    from concourse.bass_utils import run_bass_kernel_spmd as _run

    nc = _bacc.Bacc("TRN2", target_bir_lowering=False, num_devices=1)
    arrays, args, tabs = {}, [], {}
    for name in _INS:
        a = _np.ascontiguousarray(inputs[name])
        arrays[f"in_{name}_dram"] = a
        args.append(nc.dram_tensor(f"in_{name}_dram", a.shape, _mybir.dt.from_np(a.dtype), kind="ExternalInput").ap())
    for name, a in transform_tables().items():
        arrays[f"table_{name}_dram"] = a
        tabs[name] = nc.dram_tensor(f"table_{name}_dram", a.shape, _mybir.dt.float32, kind="ExternalInput").ap()
    out = nc.dram_tensor("out_0_dram", (B, L, D), _mybir.dt.float32, kind="ExternalOutput").ap()
    build_program(nc, *args, tabs, out)
    r = _run(nc, [arrays], core_ids=[0])
    return r.results[0]["out_0_dram"]
```

```python
from contextlib import ExitStack

import numpy as np

import concourse.bass as bass
from concourse import mybir

F32 = mybir.dt.float32
F32R = mybir.dt.float32r
ALU = mybir.AluOpType
ACT = mybir.ActivationFunctionType

B, L, D = 8, 512, 2048
P = 128
CH = 512
GPB = D // CH
GROUPS = B * GPB
LT = L // P
CT = CH // P
TOPK = 12
NEG = -3.0e38
EPS = 1e-5
NFFN, EXPERTS, RANK, RDIM, TOPE = 512, 64, 8, 16, 16
SCALING = 2.0
TOKENS = B * L
TT = TOKENS // P
KD = D // P
KN = NFFN // P


def transform_tables():
    H = L // 2
    p = np.arange(P)
    cos, sin, pi = np.cos, np.sin, np.pi

    def alt(n):
        return 1.0 - 2.0 * (n % 2)

    cyc = [2 * p, 2 * p + 1]
    neg = [8 * p + 1, 8 * p + 5]
    fwd = []
    for par in range(2):
        for fn in (cos, sin):
            for half in range(2):
                n = p + P * half
                m = fn(2 * pi * np.outer(n + 0.5, cyc[par]) / L)
                if par == 0 and fn is sin:
                    m[:, 0] = alt(n)
                fwd.append(m)
    for par in range(2):
        th = 2 * pi * np.outer(p + 0.5, neg[par]) / (2 * L)
        fwd += [cos(th), sin(th), -sin(th)]
    for half in range(2):
        m = cos(2 * pi * np.outer(p + P * half + 0.5, cyc[0]) / L)
        m[:, 0] = 0.0
        fwd.append(m)
    lags = []
    for par in range(2):
        even = 2.0 * cos(2 * pi * np.outer(cyc[par], np.arange(H + 1)) / L) / L
        if par == 0:
            even[0] = alt(np.arange(H + 1)) / L
        odd = 2.0 * sin(2 * pi * np.outer(cyc[par], np.arange(H)) / L) / L
        odd[:, 0] = 0.0
        if par == 0:
            odd[0] = 0.0
        lags += [even[:, :H] - even[:, H:], odd]
    wts = []
    for par in range(2):
        for fn in (cos, sin):
            for half in range(2):
                f = cyc[par].copy()
                if par == 0:
                    f[0] = H
                m = fn(2 * pi * np.outer(p + P * half, f) / L)
                if fn is cos:
                    m -= 1.0
                    if half == 0:
                        m[0] = alt(f) - 1.0
                elif half == 0:
                    m[0] = 0.0
                if par == 0 and fn is sin:
                    m[:, 0] = 0.0
                wts.append(m)
    for par in range(2):
        for fn in (cos, sin):
            for half in range(2):
                m = fn(2 * pi * np.outer(p + P * half, neg[par]) / (2 * L))
                if half == 0 and fn is sin:
                    m[0] = sin(pi * neg[par] / 2)
                wts.append(m)
    back = []
    for half in range(2):
        t = p + P * half + 0.5
        for par in range(2):
            m = 2.0 * cos(2 * pi * np.outer(cyc[par], t) / L) / (2 * L)
            if par == 0:
                m[0] /= 2
            back.append(m)
        for par in range(2):
            back.append(2.0 * sin(2 * pi * np.outer(neg[par], t) / (2 * L)) / (2 * L))
        for par in range(2):
            m = 2.0 * sin(2 * pi * np.outer(cyc[par], t) / L) / (2 * L)
            if par == 0:
                m[0] = alt(p) / (2 * L)
            back.append(m)
        for par in range(2):
            back.append(2.0 * cos(2 * pi * np.outer(neg[par], t) / (2 * L)) / (2 * L))

    def cat(ms):
        return np.ascontiguousarray(np.concatenate(ms, 1).astype(np.float32))

    return {
        "fwd": cat(fwd), "lags": cat(lags), "wts": cat(wts), "back": cat(back),
        "ident": np.eye(P, dtype=np.float32), "flip": np.ascontiguousarray(np.eye(P, dtype=np.float32)[::-1]),
    }


def attention_phase(nc, sems, x, ctx, tables, x2, rstd2, shift2):
    with ExitStack() as st:
        def sb(name, shape, dt=F32):
            return st.enter_context(nc.sbuf_tensor(name, shape, dt))

        def ps(name, shape):
            return st.enter_context(nc.psum_tensor(name, shape, F32))

        def sem(name):
            return sems.enter_context(nc.semaphore(name))

        fwd = sb("fwd", [P, 16, P])
        wts_hi, wts_lo = sb("wts_hi", [P, 16, P], F32R), sb("wts_lo", [P, 16, P], F32R)
        lags_hi, lags_lo = sb("lags_hi", [P, 2, L], F32R), sb("lags_lo", [P, 2, L], F32R)
        back_hi, back_lo = sb("back_hi", [P, 16, P], F32R), sb("back_lo", [P, 16, P], F32R)
        ident, flip = sb("ident", [P, P]), sb("flip", [P, P])
        stat_in = sb("stat_in", [P, 2, CH])
        bn_x, bn_x2 = sb("bn_x", [P, LT, GPB, 6]), sb("bn_x2", [P, LT, GPB, 6])
        norm_x = [sb(f"norm_x{n}", [P, LT, 2]) for n in range(4)]
        norm_x2 = [sb(f"norm_x2{n}", [P, LT, 2]) for n in range(4)]
        pace, zero = sb("pace", [P, 33]), sb("zero", [P, 1])
        rstd, shift = sb("rstd", [P, B * LT]), sb("shift", [P, B * LT])
        xq = sb("xq", [P, LT, CH])
        q_sum = sb("q_sum", [P, 2, CH])
        v = sb("v", [P, LT, CH])
        v_last, v_last2 = sb("v_last", [P, CH]), sb("v_last2", [P, CH])
        v_fold = sb("v_fold", [P, LT, CH])
        v_cyc = sb("v_cyc", [P, 2, 4, CH])
        v_neg = sb("v_neg", [P, 4, CH])
        prod, prod_b = sb("prod", [P, 4, CH]), sb("prod_b", [P, 2, CH])
        p_hi, p_lo = sb("p_hi", [P, 4, CH], F32R), sb("p_lo", [P, 4, CH], F32R)
        r_hi, r_lo = sb("r_hi", [P, 8, CH], F32R), sb("r_lo", [P, 8, CH], F32R)
        top = sb("top", [P, CT, 16])
        neg_max, exp_sum, inv_sum = sb("neg_max", [P, CT]), sb("exp_sum", [P, CT]), sb("inv_sum", [P, CT])
        exp_top = sb("exp_top", [P, CT, TOPK])
        e = sb("e", [P, CT, L])
        pick = sb("pick", [P, CT, L])
        w_hi = sb("w_hi", [P, LT, CH], F32R)
        w_lo = [r_hi[:, 2, :], r_hi[:, 3, :], r_lo[:, 2, :], r_lo[:, 3, :]]
        xr = sb("xr", [P, LT, CH])
        rev = sb("rev", [P, 2, CH])

        pair_ps = [[ps(f"pair{s}{n}", [P, CH]) for n in "ab"] for s in range(2)]
        lag_ps = [ps(f"lag{s}", [P, L]) for s in range(2)]
        evac_ps = [ps(f"evac{s}", [P, CH]) for s in range(2)]

        start_loaded, fwd_loaded, tables_loaded, tables_split = sem("start_loaded"), sem("fwd_loaded"), sem("tables_loaded"), sem("tables_split")
        stat_loaded, stat_used = [sem(f"stat_loaded{n}") for n in range(2)], sem("stat_used")
        x_norm_step, x_sqrt_done, x_norm_ready = sem("x_norm_step"), sem("x_sqrt_done"), sem("x_norm_ready")
        x2_stat, x2_norm_step, x2_sqrt_done, x2_norm_ready = (
            sem("x2_stat"), sem("x2_norm_step"), sem("x2_sqrt_done"), sem("x2_norm_ready"))
        xq_loaded, v_loaded, xr_loaded = sem("xq_loaded"), sem("v_loaded"), sem("xr_loaded")
        normed, q_folded = sem("normed"), sem("q_folded")
        v_folded, v_halves, v_shifted, v_twisted = sem("v_folded"), sem("v_halves"), sem("v_shifted"), sem("v_twisted")
        evac_ready, evac_done, w_lo_done = sem("evac_ready"), sem("evac_done"), sem("w_lo_done")
        pair_ready, pair_done = sem("pair_ready"), sem("pair_done")
        prod_ready, prod_added, sum_ready = sem("prod_ready"), sem("prod_added"), sem("sum_ready")
        hi_done, lo_done = sem("hi_done"), sem("lo_done")
        last_scaled, dc_done = sem("last_scaled"), sem("dc_done")
        lag_ready, corr_summed, topk_step, exp_done = sem("lag_ready"), sem("corr_summed"), sem("topk_step"), sem("exp_done")
        odd_copied = sem("odd_copied")
        inv_done, picked, weighted, w_folded = sem("inv_done"), sem("picked"), sem("weighted"), sem("w_folded")
        even_copied, rev_ready, x2_step, flip_used, stored = (
            sem("even_copied"), sem("rev_ready"), sem("x2_step"), sem("flip_used"), sem("stored"))

        x_t = x.rearrange("b (j p) d -> b p j d", p=P)
        ctx_t = ctx.rearrange("b (j p) d -> b p j d", p=P)
        x2_t = x2.rearrange("b (j p) d -> p (b j) d", p=P)

        def quarter(r, off):
            return (2 + r + off) % GPB, (2 + r + off) // GPB

        def at_group(arr, k, r, off):
            q, later = quarter(r, off)
            return arr[bass.ds(k + later, 1), :, :, q * CH:(q + 1) * CH].rearrange("o p j c -> (o p) j c")

        def is_step(i, n):
            return isinstance(i, int) and i == n

        def evac_cyc(i, n):
            return n if is_step(i, 0) else 12 * i - 4 + n

        def evac_wt(i, n):
            return 12 * i + n - (4 if is_step(i, GROUPS) else 0)

        def evac_neg(i, n):
            return 12 * i + 4 + n

        def pair_q(i, n):
            return n if is_step(i, 0) else 8 * i - 6 + n

        def pair_w(i, n):
            return 8 * i - 4 + n - (2 if is_step(i, GROUPS) else 0)

        def pair_o(i, n):
            return 8 * i + n - (2 if is_step(i, GROUPS) else 0)

        def half_p(i, n):
            return n if is_step(i, 0) else 12 * i - 8 + n

        def slot_p(i, n):
            return n % 4

        def half_r(i, n):
            return 12 * i - 4 + n - (4 if is_step(i, GROUPS) else 0)

        def slot_r(i, n):
            return n % 4

        def lag_flip(i, n):
            return 6 * i - 4 + n - (4 if is_step(i, GROUPS + 1) else 0)

        def lag_corr(i, n):
            return n if is_step(i, 0) else 6 * i - 2 + n

        def corr_at(i, c, second):
            return 8 * i + 4 * (c // 2) + 2 * second + c % 2 + 1

        def topk_at(i, c, stage):
            return 24 * i + 12 * (c // 2) + 2 * stage + c % 2 + 1

        def exp_at(i, c, small):
            return 8 * i + 4 * (c // 2) + 2 * small + c % 2 + 1

        W_BLOCKS = (2, 3, 0, 1)

        def steps(eng, body):
            body(-1, 2, True, False, False, True)
            body(-1, 3, True, True, False, True)
            with eng.Fori(0, B - 1) as k:
                for r in range(4):
                    body(k, r, True, True, True, True)
            body(B - 1, 0, True, True, True, True)
            body(B - 1, 1, True, True, True, False)
            body(B - 1, 2, False, True, True, False)
            body(B - 1, 3, False, False, True, False)

        def has_stats(k, r):
            return r < 2 and not isinstance(k, int)

        def stat_at(k, r, n):
            return 16 * k + 8 * r + n

        block = st.enter_context(nc.Block())

        @block.sync
        def _(sp):
            def whole(buf):
                return buf[:, 0].rearrange("p j c -> p (j c)") if buf is v_cyc else buf[:].rearrange("p j c -> p (j c)")

            def load_xq(k, r, off):
                sp.dma_start(xq[:], at_group(x_t, k, r, off)).then_inc(xq_loaded, 16)

            def load_v(k, r, off, last_used):
                q, later = quarter(r, off)
                sp.dma_start(v[:], at_group(ctx_t, k, r, off)).then_inc(v_loaded, 16)
                if last_used is not None:
                    sp.wait_ge(dc_done, last_used)
                last = ctx[bass.ds(k + later, 1), L - 1:L, q * CH:(q + 1) * CH].rearrange("o p c -> (o p) c")
                sp.dma_start(v_last[:], last.broadcast_to((P, CH))).then_inc(v_loaded, 16)

            load_v(-1, 2, 0, None)
            for j, buf in enumerate((pick, e, v_cyc, xr)):
                sp.dma_start(whole(buf), x[0, j * P:(j + 1) * P, :]).then_inc(start_loaded, 16)

            load_xq(-1, 2, 0)
            sp.dma_start(fwd[:].rearrange("p n m -> p (n m)"), tables["fwd"]).then_inc(fwd_loaded, 16)
            sp.dma_start(ident[:], tables["ident"]).then_inc(tables_loaded, 16)
            sp.dma_start(flip[:], tables["flip"]).then_inc(tables_loaded, 16)
            sp.dma_start(v_neg[:, 0:2, :].rearrange("p n c -> p (n c)"), tables["lags"]).then_inc(tables_loaded, 16)
            sp.dma_start(v_cyc[:, 1].rearrange("p n c -> p (n c)"), tables["wts"]).then_inc(tables_loaded, 16)
            sp.wait_ge(stat_used, 1)
            sp.dma_start(pick[:].rearrange("p n c -> p (n c)"), tables["back"]).then_inc(tables_loaded, 16)

            def body(k, r, a, b, c, f):
                i = 4 * k + 2 + r

                def stat_pair(m):
                    if has_stats(k, r):
                        for h in range(2):
                            n = stat_at(k, r, 2 * m + h)
                            if not (m < 1 and r == 0):
                                sp.wait_ge(stat_used, n)
                            tile, q = (8 * r + 2 * m + h) // GPB, (2 * m + h) % GPB
                            sp.dma_start(stat_in[:, h, :], x[bass.ds(k + 1, 1), tile * P:(tile + 1) * P, q * CH:(q + 1) * CH]
                                         .rearrange("o p c -> (o p) c")).then_inc(stat_loaded[h], 16)

                if has_stats(k, r) and r == 0:
                    sp.wait_ge(x_norm_ready, 2 * (k + 1))
                stat_pair(0)
                if f:
                    sp.wait_ge(pair_ready, pair_q(i, 1) + 1)
                    load_xq(k, r, 1)
                stat_pair(1)
                if f:
                    sp.wait_ge(v_twisted, 2 * i + 2)
                    load_v(k, r, 1, i + 1)
                stat_pair(2)
                stat_pair(3)
                if c:
                    sp.wait_ge(x2_stat, LT * (i - 1))
                    sp.dma_start(x2_t[:, bass.ds(LT * k, LT), r * CH:(r + 1) * CH], xr[:]).then_inc(stored, 16)
                if b:
                    if c:
                        sp.wait_ge(stored, 16 * (i - 1))
                    else:
                        sp.wait_ge(x_norm_ready, 2)
                    sp.dma_start(xr[:], at_group(x_t, k, r, -1)).then_inc(xr_loaded, 16)

            steps(sp, body)
            sp.wait_ge(stored, 16 * GROUPS)

        @block.tensor
        def _(pe):
            def fwd_mm(out, n, rhs, start, stop):
                return nc.tensor.matmul(out[:], fwd[:, n, :], rhs, start=start, stop=stop)

            def split_mm(out, lhs_hi, lhs_lo, rhs_hi, rhs_lo, start, stop):
                nc.tensor.matmul(out, lhs_hi, rhs_hi, start=start, stop=False)
                nc.tensor.matmul(out, lhs_hi, rhs_lo, start=False, stop=False)
                return nc.tensor.matmul(out, lhs_lo, rhs_hi, start=False, stop=stop)

            pe.wait_ge(fwd_loaded, 16)

            def body(k, r, a, b, c, f):
                i = 4 * k + 2 + r
                if a:
                    pe.wait_ge(v_folded, i + 1)
                    for n in range(4):
                        if not (is_step(i, 0) and n < 2):
                            pe.wait_ge(evac_done, evac_cyc(i, n) - 1)
                        bank = evac_ps[n % 2]
                        for h in range(2):
                            last = fwd_mm(bank, 2 * n + h, v_fold[:, 2 * (n // 2) + h, :], h == 0, h == 1)
                        last.then_inc(evac_ready, 1)
                def x_spectrum(n):
                    pe.wait_ge(q_folded, 2 * i + n + 1)
                    if b:
                        pe.wait_ge(pair_done, 2 * (i - 1) + n + 1)
                    bank = pair_ps[n % 2]
                    src = q_sum if n == 0 else xq
                    for h in range(2):
                        fwd_mm(bank[0], 14 + h if n == 0 else 4 + h, src[:, h, :], h == 0, h == 1)
                    for h in range(2):
                        last = fwd_mm(bank[1], 4 * n + 2 + h, src[:, h, :], h == 0, h == 1)
                    last.then_inc(pair_ready, 1)

                def turn_weights(tiles):
                    pe.wait_ge(w_folded, 3 * CT * i)
                    for l in tiles:
                        if l < 2:
                            pe.wait_ge(evac_done, evac_wt(i, l) - 1)
                        else:
                            pe.wait_ge(w_lo_done, LT * (i - 1) + l - 1)
                        for t in range(CT):
                            last = nc.tensor.transpose(evac_ps[l % 2][:, t * P:(t + 1) * P],
                                                       pick[:, t, l * P:(l + 1) * P], ident[:])
                        last.then_inc(evac_ready, 1)

                if a:
                    x_spectrum(0)
                if c:
                    for h in range(2):
                        if a or b:
                            pe.wait_ge(corr_summed, corr_at(i - 1, 2 + h, 1))
                        else:
                            pe.wait_ge(flip_used, 2 * (i - 3) + h + 1)
                        pe.wait_ge(rev_ready, 2 * (i - 2) + h + 1)
                        nc.tensor.matmul(lag_ps[h][:], flip[:], rev[:, h, :], start=True, stop=True).then_inc(lag_ready, 1)
                if b:
                    turn_weights((0, 1))
                if a:
                    x_spectrum(1)
                if b:
                    turn_weights((2, 3))
                def weights_spectrum(n):
                    blk = W_BLOCKS[n]
                    if n >= 2:
                        pe.wait_ge(prod_ready, half_r(i, 2 * n - 3) + 1)
                    elif a:
                        pe.wait_ge(prod_ready, half_p(i, 2 * n + 1) + 1)
                    else:
                        pe.wait_ge(pair_done, 2 * (i - 1) + n + 1)
                    cos_in, sin_in = (0, 2) if blk < 2 else (2, 0)
                    bank = pair_ps[n % 2]
                    for part, first in sorted(enumerate((cos_in, sin_in)), key=lambda pf: pf[1]):
                        if n == 0:
                            pe.wait_ge(evac_done, evac_wt(i, first + 1) + 1)
                            pe.wait_ge(w_lo_done, LT * (i - 1) + first + 2)
                        for h in range(2):
                            t = 4 * blk + 2 * part + h
                            last = split_mm(bank[part][:], wts_hi[:, t, :], wts_lo[:, t, :],
                                            w_hi[:, first + h, :], w_lo[first + h], h == 0, h == 1)
                    last.then_inc(pair_ready, 1)

                def ctx_twisted(n):
                    pe.wait_ge(v_twisted, 2 * i + n // 2 + 1)
                    if b and n < 2:
                        pe.wait_ge(w_lo_done, LT * (i - 1) + n + 3)
                    else:
                        pe.wait_ge(evac_done, evac_neg(i, n) - 1)
                    bank = evac_ps[n % 2]
                    re, im = (1, 3) if n < 2 else (0, 2)
                    t = 8 + 3 * (n // 2)
                    fwd_mm(bank, t + (n % 2), v_fold[:, re, :], True, False)
                    fwd_mm(bank, t + (2 if n % 2 == 0 else 0), v_fold[:, im, :], False, True).then_inc(evac_ready, 1)

                for pair in ((0, 1), (2, 3)):
                    if b:
                        for n in pair:
                            weights_spectrum(n)
                    if a:
                        for n in pair:
                            ctx_twisted(n)

                def corr(tiles):
                    pe.wait_ge(hi_done, half_p(i, 3) + 1)
                    pe.wait_ge(lo_done, half_p(i, 3) + 1)
                    if is_step(i, 0):
                        pe.wait_ge(tables_split, 6)
                    for t in tiles:
                        if t >= 2:
                            pe.wait_ge(corr_summed, corr_at(i, t - 2, 1))
                        elif c:
                            pe.wait_ge(flip_used, 2 * (i - 2) + t + 1)
                        elif b:
                            pe.wait_ge(corr_summed, corr_at(i - 1, 2 + t, 1))
                        ch = slice(t * P, (t + 1) * P)
                        for part, cols in enumerate((slice(0, L // 2), slice(L // 2, L))):
                            for par in range(2):
                                row = 2 * par + part
                                last = split_mm(lag_ps[t % 2][:, cols], p_hi[:, row, ch], p_lo[:, row, ch],
                                                lags_hi[:, par, cols], lags_lo[:, par, cols], par == 0, par == 1)
                        last.then_inc(lag_ready, 1)

                def out(h):
                    pe.wait_ge(prod_ready, half_r(i, 5 + 2 * h) + 1)
                    for made, turn in ((3, 0), (5, 1), (7, 2)):
                        pe.wait_ge(hi_done, half_r(i, made) + 1)
                        pe.wait_ge(lo_done, half_r(i, made) + 1)
                        for part, rows in enumerate(((0, 2, 5, 7), (1, 3, 4, 6))):
                            for row in ((rows[2:], rows[:1], rows[1:2])[turn]):
                                t = 8 * h + 4 * part + rows.index(row)
                                last = split_mm(pair_ps[h][part][:], back_hi[:, t, :], back_lo[:, t, :],
                                                r_hi[:, row, :], r_lo[:, row, :], row == rows[2], row == rows[1])
                    last.then_inc(pair_ready, 1)

                for h in range(2):
                    if a:
                        corr((2 * h, 2 * h + 1))
                    if b:
                        out(h)

            steps(pe, body)

        @block.vector
        def _(dve):
            held = [0]

            def hold(sem_, value):
                dve.wait_ge(sem_, value)
                nc.vector.memset(pace[:, held[0] % 32:held[0] % 32 + 1], 0.0)
                held[0] += 1

            def norm_begin(bn, tmp, step, n):
                mv, ve = tmp[0], tmp[1]
                for j in range(LT):
                    nc.vector.bn_aggr(mv[:, j, :], bn[:, j, :, :].rearrange("p g s -> p (g s)")).then_inc(step, 1)
                dve.wait_ge(step, 9 * n + 4)
                nc.vector.tensor_scalar(ve[:, :, 0], mv[:, :, 1], EPS, None, ALU.add).then_inc(step, 1)

            def norm_end(tmp, step, sqrt_done, n, scale, shift_, ready):
                mv, ve, sd, t = tmp
                y0, t = sd[:, :, 1], t[:, :, 0]
                cols = bass.ds(LT * n, LT)
                dve.wait_ge(sqrt_done, n + 1)
                nc.vector.reciprocal(y0, sd[:, :, 0]).then_inc(step, 1)
                dve.wait_ge(step, 9 * n + 6)
                nc.vector.tensor_tensor(t, ve[:, :, 0], y0, ALU.mult).then_inc(step, 1)
                dve.wait_ge(step, 9 * n + 7)
                nc.vector.tensor_tensor(t, t, y0, ALU.mult).then_inc(step, 1)
                dve.wait_ge(step, 9 * n + 8)
                nc.vector.tensor_scalar(t, t, -0.5, 1.5, ALU.mult, ALU.add).then_inc(step, 1)
                dve.wait_ge(step, 9 * n + 9)
                nc.vector.tensor_tensor(scale[:, cols], t, y0, ALU.mult).then_inc(ready, 1)
                dve.wait_ge(ready, 2 * n + 1)
                nc.vector.scalar_tensor_tensor(shift_[:, cols], mv[:, :, 0], -1.0, scale[:, cols],
                                               ALU.mult, ALU.mult).then_inc(ready, 1)

            def low_half(n, buf, slot, row):
                dve.wait_ge(hi_done, n + 1)
                nc.vector.tensor_tensor(buf[:, row, :], prod[:, slot, :],
                                        (p_hi if buf is p_lo else r_hi)[:, row, :].bitcast(F32), ALU.subtract).then_inc(lo_done, 1)

            def products(blocks, half, slot_of, pair, spec_of, buf, spec_wait, weights, after):
                count = 2 * len(blocks)
                for n in range(count):
                    blk = blocks[n // 2]
                    c_ps, s_ps = pair_ps[(n // 2) % 2]
                    c_v, s_v = spec_of(blk)
                    if n % 2 == 0:
                        dve.wait_ge(pair_ready, pair(n // 2) + 1)
                        spec_wait(blk)
                    slot = slot_of(n)
                    if not (isinstance(half(n), int) and half(n) < 4):
                        dve.wait_ge(lo_done, half(n) - 3)
                    first_v, second_v = (c_v, s_v) if n % 2 == 0 else (s_v, c_v)
                    def added():
                        if not (isinstance(half(n), int) and half(n) < 2):
                            dve.wait_ge(sum_ready, half(n) - 1)

                    if not weights and n % 2 == 1:
                        nc.vector.tensor_tensor(prod[:, slot, :], s_ps[:], c_v, ALU.mult)
                        added()
                        op = nc.vector.tensor_tensor(prod_b[:, slot % 2, :], c_ps[:], s_v, ALU.mult)
                    else:
                        if weights and blk < 2:
                            nc.vector.scalar_tensor_tensor(prod[:, slot, :], c_ps[:], 1.0, first_v, ALU.add, ALU.mult)
                        else:
                            nc.vector.tensor_tensor(prod[:, slot, :], c_ps[:], first_v, ALU.mult)
                        added()
                        op = nc.vector.tensor_tensor(prod_b[:, slot % 2, :], s_ps[:], second_v, ALU.mult)
                    op.then_inc(prod_ready, 1)
                    after(n)

            dve.wait_ge(start_loaded, 16 * LT)
            for j, buf in enumerate((pick, e, v_cyc, xr)):
                for q in range(GPB):
                    op = nc.vector.bn_stats(bn_x[:, j, q, :], buf[:, 0, q, :] if buf is v_cyc else buf[:, q, :])
            op.then_inc(stat_used, 1)
            dve.wait_ge(stat_used, 1)
            norm_begin(bn_x, norm_x, x_norm_step, 0)
            norm_end(norm_x, x_norm_step, x_sqrt_done, 0, rstd, shift, x_norm_ready)
            def split_tables():
                dve.wait_ge(tables_loaded, 16 * 5)
                dve.wait_ge(tables_split, 3)
                nc.vector.tensor_tensor(lags_lo[:], v_neg[:, 0:2, :], lags_hi[:].bitcast(F32), ALU.subtract).then_inc(tables_split, 1)
                for lo, hi, src in ((wts_lo, wts_hi, v_cyc[:, 1]), (back_lo, back_hi, pick)):
                    nc.vector.tensor_tensor(lo[:].rearrange("p n m -> p (n m)"), src[:].rearrange("p n c -> p (n c)"),
                                            hi[:].rearrange("p n m -> p (n m)").bitcast(F32), ALU.subtract).then_inc(tables_split, 1)

            def body(k, r, a, b, c, f):
                i = 4 * k + 2 + r
                cyc, cyc_before = r % 2, (r + 1) % 2

                def stat_pair(m):
                    if has_stats(k, r):
                        for h in range(2):
                            tile, q = (8 * r + 2 * m + h) // GPB, (2 * m + h) % GPB
                            dve.wait_ge(stat_loaded[h], 16 * (8 * k + 4 * r + m + 1))
                            nc.vector.bn_stats(bn_x[:, tile, q, :], stat_in[:, h, :]).then_inc(stat_used, 1)

                def weights_low(tiles):
                    for l in tiles:
                        if b:
                            dve.wait_ge(evac_done, evac_wt(i, l) + 1)
                            nc.vector.tensor_tensor(w_lo[l], evac_ps[l % 2][:], w_hi[:, l, :].bitcast(F32),
                                                    ALU.subtract).then_inc(w_lo_done, 1)

                stat_pair(0)
                if not a:
                    weights_low(range(LT))
                def add_turned():
                    for h in range(2):
                        dve.wait_ge(lag_ready, lag_flip(i, h) + 1)
                        nc.vector.tensor_tensor(xr[:, 3 - h, :], lag_ps[h][:], xr[:, 3 - h, :], ALU.add).then_inc(flip_used, 1)

                def corr_low(n):
                    low_half(half_p(i, n), p_lo, slot_p(i, n), n)

                def after_corr(n):
                    if n == 1:
                        weights_low((0, 1))
                    if n == 2:
                        weights_low((2, 3))
                    if n == 3:
                        corr_low(0)
                        corr_low(1)

                if a:
                    products((0, 1), lambda n: half_p(i, n), lambda n: slot_p(i, n), lambda n: pair_q(i, n),
                             lambda blk: (v_cyc[:, cyc, 2 * blk, :], v_cyc[:, cyc, 2 * blk + 1, :]), p_lo,
                             lambda blk: dve.wait_ge(evac_done, evac_cyc(i, 2 * blk + 1) + 1), False,
                             after_corr)
                    if not b:
                        corr_low(2)
                        corr_low(3)
                        nc.vector.memset(pace[:, 32:33], 0.0).then_inc(pair_done, 2)
                        split_tables()
                def x2_statistics():
                    dve.wait_ge(pair_done, 2 * i)
                    for j in range(LT):
                        if j == 2:
                            dve.wait_ge(flip_used, 2 * (i - 1))
                        nc.vector.bn_stats(bn_x2[:, j, r, :], xr[:, j, :]).then_inc(x2_stat, 1)
                    if r == 3:
                        hold(x2_stat, LT * (i - 1))
                        norm_begin(bn_x2, norm_x2, x2_norm_step, k)

                if c and not b:
                    add_turned()
                if b:
                    dve.wait_ge(dc_done, i)

                    def spec_wait(blk):
                        if blk >= 2:
                            dve.wait_ge(evac_done, evac_neg(i - 1, 2 * (blk - 2) + 1) + 1)

                    def out_low(n):
                        low_half(half_r(i, n), r_lo, slot_r(i, n), 2 * W_BLOCKS[n // 2] + n % 2)

                    def after_out(n):
                        if n == 1 and a:
                            corr_low(2)
                        if n == 1 and not a:
                            out_low(0)
                            out_low(1)
                        if n == 2 and a:
                            corr_low(3)
                        if n == 3 and a:
                            out_low(0)
                            out_low(1)
                        if n >= 4:
                            out_low(n - 2)
                        if n == 3:
                            if c:
                                add_turned()

                    products(W_BLOCKS, lambda n: half_r(i, n), lambda n: slot_r(i, n), lambda n: pair_w(i, n),
                             lambda blk: ((v_cyc[:, cyc_before, 2 * blk, :], v_cyc[:, cyc_before, 2 * blk + 1, :]) if blk < 2
                                          else (v_neg[:, 2 * blk - 4, :], v_neg[:, 2 * blk - 3, :])), r_lo,
                             spec_wait, True, after_out)
                    out_low(6)
                    stat_pair(1)
                    out_low(7)
                if a:
                    def sums(t, second):
                        even, odd = lag_ps[t % 2][:, 0:L // 2], e[:, t, L // 2:L]
                        if not second:
                            dve.wait_ge(odd_copied, CT * i + t + 1)
                            op = nc.vector.tensor_tensor(e[:, t, 0:L // 2], even, odd, ALU.add)
                        else:
                            dve.wait_ge(corr_summed, corr_at(i, t, 0))
                            op = nc.vector.tensor_tensor(odd[:, 1:], even[:, 1:], odd[:, 1:], ALU.subtract)
                        op.then_inc(corr_summed, 1)

                    def topk(t, stage):
                        if stage == 0:
                            hold(corr_summed, corr_at(i, t, 1))
                            op = nc.vector.max(top[:, t, 0:8], e[:, t, :])
                        elif stage == 1:
                            dve.wait_ge(topk_step, topk_at(i, t, 0))
                            op = nc.vector.tensor_scalar(neg_max[:, t:t + 1], top[:, t, 0:1], -1.0, None, ALU.mult)
                        elif stage == 2:
                            op = nc.vector.match_replace(pick[:, t, :], top[:, t, 0:8], e[:, t, :], NEG)
                        elif stage == 3:
                            hold(topk_step, topk_at(i, t, 2))
                            op = nc.vector.max(top[:, t, 8:16], pick[:, t, :])
                        elif stage == 4:
                            dve.wait_ge(topk_step, topk_at(i, t, 3))
                            op = nc.vector.memset(top[:, t, TOPK:16], NEG)
                        else:
                            hold(topk_step, topk_at(i, t, 4))
                            op = nc.vector.match_replace(pick[:, t, :], top[:, t, 8:16], pick[:, t, :], NEG)
                        op.then_inc(topk_step, 1)

                    def choose(t):
                        dve.wait_ge(exp_done, exp_at(i, t, True))
                        nc.vector.reciprocal(inv_sum[:, t:t + 1], exp_sum[:, t:t + 1]).then_inc(inv_done, 1)
                        dve.wait_ge(topk_step, topk_at(i, t, 5))
                        nc.vector.scalar_tensor_tensor(e[:, t, :], pick[:, t, :], NEG, e[:, t, :],
                                                       ALU.is_equal, ALU.mult).then_inc(picked, 1)

                def residual(h):
                    n = 2 * (i - 1) + h
                    odd = pair_ps[h][1]
                    dve.wait_ge(x2_step, n + 1)
                    nc.vector.tensor_tensor(rev[:, h, :], rev[:, h, :], odd[:], ALU.subtract).then_inc(rev_ready, 1)
                    nc.vector.tensor_tensor(xr[:, h, :], odd[:], xr[:, h, :], ALU.add).then_inc(pair_done, 1)

                def sums_of(pair):
                    for second in (0, 1):
                        for t in pair:
                            sums(t, second)

                if a:
                    sums_of((0, 1))
                if c:
                    x2_statistics()
                stat_pair(2)
                if a:
                    for stage in range(6):
                        if stage == 5 and has_stats(k, r) and r == 1:
                            norm_end(norm_x, x_norm_step, x_sqrt_done, k + 1, rstd, shift, x_norm_ready)
                        for t in (0, 1):
                            topk(t, stage)
                        if stage == 3:
                            stat_pair(3)
                            if has_stats(k, r) and r == 1:
                                hold(stat_used, 16 * k + 17)
                                norm_begin(bn_x, norm_x, x_norm_step, k + 1)
                    sums_of((2, 3))
                    for stage in range(5):
                        for t in (2, 3):
                            topk(t, stage)
                        if stage == 2:
                            choose(0)
                            choose(1)
                        if stage == 3 and b:
                            residual(0)
                    for t in (2, 3):
                        topk(t, 5)
                        choose(t)
                elif b:
                    residual(0)
                if b:
                    residual(1)
                if has_stats(k, r) and r == 1:
                    dve.wait_ge(q_folded, 2 * i + 3)
                    nc.vector.tensor_tensor(xq[:, 0:2, :], xq[:, 0:2, :], xq[:, 2:4, :], ALU.subtract).then_inc(q_folded, 1)
                if c and r == 3:
                    norm_end(norm_x2, x2_norm_step, x2_sqrt_done, k, rstd2, shift2, x2_norm_ready)

            steps(dve, body)

        @block.scalar
        def _(act):
            def norm_inputs(k, r, off):
                act.wait_ge(xq_loaded, 16 * (4 * k + 2 + r + off) + 16)
                act.wait_ge(x_norm_ready, 2 * (k + quarter(r, off)[1]) + 2)

            def norm(k, r, off, tiles):
                batch = k + quarter(r, off)[1]
                for j in tiles:
                    t = bass.ds(LT * batch + j, 1)
                    nc.scalar.activation(xq[:, j, :], xq[:, j, :], ACT.Identity, bias=shift[:, t], scale=rstd[:, t]).then_inc(normed, 1)

            def halves(i):
                act.wait_ge(v_folded, i + 1)
                for tile, src in ((1, 3), (3, 1)):
                    nc.scalar.activation(v[:, tile, :], v_fold[:, src, :], ACT.Copy, scale=0.5 ** 0.5).then_inc(v_halves, 1)
                nc.scalar.activation(v_last2[:], v_last[:], ACT.Copy, scale=2.0 ** 0.5).then_inc(v_halves, 1)

            def weigh(i, t):
                act.wait_ge(inv_done, CT * i + t + 1)
                act.wait_ge(picked, CT * i + t + 1)
                nc.scalar.activation(e[:, t, :], e[:, t, :], ACT.Copy, scale=inv_sum[:, t:t + 1]).then_inc(weighted, 1)

            def high_half(n, buf, slot, row):
                act.wait_ge(sum_ready, n + 1)
                nc.scalar.activation(buf[:, row, :], prod[:, slot, :], ACT.Copy).then_inc(hi_done, 1)

            def evac(n, dst, src):
                act.wait_ge(evac_ready, n + 1)
                nc.scalar.activation(dst, src[:], ACT.Copy).then_inc(evac_done, 1)

            def sqrt(tmp, step, done, n):
                act.wait_ge(step, 9 * n + 5)
                nc.scalar.activation(tmp[2][:, :, 0], tmp[1][:, :, 0], ACT.Sqrt).then_inc(done, 1)

            sqrt(norm_x, x_norm_step, x_sqrt_done, 0)
            norm_inputs(-1, 2, 0)
            norm(-1, 2, 0, range(LT))
            halves(0)
            def split_tables():
                act.wait_ge(tables_loaded, 16 * 5)
                nc.scalar.activation(lags_hi[:], v_neg[:, 0:2, :], ACT.Copy).then_inc(tables_split, 1)
                for hi, src in ((wts_hi, v_cyc[:, 1]), (back_hi, pick)):
                    nc.scalar.activation(hi[:].rearrange("p n m -> p (n m)"), src[:].rearrange("p n c -> p (n c)"),
                                         ACT.Copy).then_inc(tables_split, 1)

            def body(k, r, a, b, c, f):
                i = 4 * k + 2 + r
                if a:
                    for n in (2,) if b else (0, 1, 2):
                        evac(evac_cyc(i, n), v_cyc[:, r % 2, n, :], evac_ps[n % 2])
                if b:
                    for t in (2, 3):
                        weigh(i - 1, t)
                if a:
                    evac(evac_cyc(i, 3), v_cyc[:, r % 2, 3, :], evac_ps[1])
                    act.wait_ge(v_shifted, 2 * i + 2)
                    act.wait_ge(v_halves, 3 * i + 3)
                    nc.scalar.activation(v_last[0:1, :], v_last[0:1, :], ACT.Copy, scale=float(L)).then_inc(last_scaled, 1)
                if not b and a:
                    split_tables()
                if b:
                    for l in (0, 1):
                        evac(evac_wt(i, l), w_hi[:, l, :], evac_ps[l % 2])
                if a:
                    for n in (0, 1):
                        high_half(half_p(i, n), p_hi, slot_p(i, n), n)
                if b:
                    for l in (2, 3):
                        evac(evac_wt(i, l), w_hi[:, l, :], evac_ps[l % 2])
                if a:
                    for n in (2, 3):
                        high_half(half_p(i, n), p_hi, slot_p(i, n), n)
                if b:
                    if c:
                        act.wait_ge(pair_ready, pair_o(i - 1, 1) + 1)
                late_norm = has_stats(k, r) and r == 1
                for what, m in (("high", 0), ("high", 1), ("neg", 0), ("high", 2), ("neg", 1), ("high", 3),
                                ("high", 4), ("high", 5), ("neg", 2), ("high", 6), ("neg", 3), ("high", 7)):
                    if b and what == "high":
                        high_half(half_r(i, m), r_hi, slot_r(i, m), 2 * W_BLOCKS[m // 2] + m % 2)
                    elif a and what == "neg":
                        if b:
                            act.wait_ge(prod_ready, half_r(i, 2 * (m // 2) + 1) + 1)
                        elif m == 0:
                            act.wait_ge(tables_split, 6)
                        if m == 3 and f and not late_norm:
                            norm_inputs(k, r, 1)
                        evac(evac_neg(i, m), v_neg[:, m, :], evac_ps[m % 2])

                def odd_copies(tiles):
                    for t in tiles:
                        act.wait_ge(lag_ready, lag_corr(i, t) + 1)
                        nc.scalar.activation(e[:, t, L // 2:L], lag_ps[t % 2][:, L // 2:L], ACT.Copy).then_inc(odd_copied, 1)

                if a:
                    odd_copies((0, 1))
                if late_norm:
                    halves(i + 1)
                    sqrt(norm_x, x_norm_step, x_sqrt_done, k + 1)
                if f and not late_norm:
                    norm(k, r, 1, range(LT))
                    halves(i + 1)
                if c and r == 3:
                    sqrt(norm_x2, x2_norm_step, x2_sqrt_done, k)
                if a:
                    odd_copies((2, 3))

                def big_exp(t):
                    act.wait_ge(topk_step, topk_at(i, t, 2))
                    nc.scalar.activation(e[:, t, :], e[:, t, :], ACT.Exp, bias=neg_max[:, t:t + 1]).then_inc(exp_done, 1)

                def top_exp(t):
                    act.wait_ge(topk_step, topk_at(i, t, 3))
                    nc.scalar.activation(exp_top[:, t, :], top[:, t, 0:TOPK], ACT.Exp, bias=neg_max[:, t:t + 1],
                                         accum_out=exp_sum[:, t:t + 1]).then_inc(exp_done, 1)

                def copy_even(h):
                    act.wait_ge(pair_ready, pair_o(i, h) + 1)
                    nc.scalar.activation(rev[:, h, :], pair_ps[h][0][:], ACT.Copy).then_inc(even_copied, 1)

                if a:
                    for t in (0, 1):
                        big_exp(t)
                    for t in (0, 1):
                        top_exp(t)
                if b:
                    copy_even(0)
                    if late_norm:
                        norm_inputs(k, r, 1)
                    copy_even(1)
                if f:
                    if b:
                        act.wait_ge(prod_ready, half_p(i + 1, 0))
                    else:
                        act.wait_ge(tables_split, 6)
                    for n in (0, 1):
                        evac(evac_cyc(i + 1, n), v_cyc[:, (r + 1) % 2, n, :], evac_ps[n])
                if late_norm:
                    norm(k, r, 1, range(LT))
                if a:
                    for t in (2, 3):
                        big_exp(t)
                    for t in (0, 1):
                        weigh(i, t)
                    for t in (2, 3):
                        top_exp(t)
            steps(act, body)

        @block.gpsimd
        def _(pool):
            def fold_v(g):
                pool.wait_ge(v_loaded, 32 * g + 32)
                nc.gpsimd.tensor_tensor(v_fold[:, 0:2, :], v[:, 0:2, :], v[:, 2:4, :], ALU.add)
                nc.gpsimd.tensor_tensor(v_fold[:, 2:4, :], v[:, 0:2, :], v[:, 2:4, :], ALU.subtract).then_inc(v_folded, 1)

            def fold_q(g, second=True):
                pool.wait_ge(normed, LT * g + LT)
                nc.gpsimd.tensor_tensor(q_sum[:], xq[:, 0:2, :], xq[:, 2:4, :], ALU.add).then_inc(q_folded, 1)
                if second:
                    nc.gpsimd.tensor_tensor(xq[:, 0:2, :], xq[:, 0:2, :], xq[:, 2:4, :], ALU.subtract).then_inc(q_folded, 1)

            def shift_v(g):
                pool.wait_ge(v_folded, g + 1)
                last = v_last[:].unsqueeze(1).broadcast_to((P, 2, CH))
                nc.gpsimd.tensor_tensor(v[:, 0:4:2, :], v[:, 0:4:2, :], last, ALU.subtract).then_inc(v_shifted, 1)
                pool.wait_ge(v_halves, 3 * g + 3)
                nc.gpsimd.tensor_tensor(v[:, 3, :], v[:, 3, :], v_last2[:], ALU.subtract).then_inc(v_shifted, 1)

            def twist_v(i, second):
                pool.wait_ge(v_shifted, 2 * i + 2)
                pool.wait_ge(evac_ready, evac_cyc(i, 3) + 1)
                op, first = (ALU.subtract, 0) if second else (ALU.add, 1)
                nc.gpsimd.tensor_tensor(v_fold[:, first:4:2, :], v[:, 0:4:2, :], v[:, 1:4:2, :], op).then_inc(v_twisted, 1)

            def add_half(n, slot, op, dc_row, dc):
                pool.wait_ge(prod_ready, n + 1)
                ins = nc.gpsimd.tensor_tensor(prod[:, slot, :], prod[:, slot, :], prod_b[:, slot % 2, :], op)
                if dc_row is not None:
                    ins.then_inc(prod_added, 1)
                    pool.wait_ge(prod_added, dc)
                    ins = nc.gpsimd.tensor_tensor(prod[0:1, slot, :], dc_row, zero[0:1, :].broadcast_to((1, CH)), ALU.add)
                ins.then_inc(sum_ready, 1)

            def fold_w(i, t):
                pool.wait_ge(weighted, CT * i + t + 1)
                up, down = e[:, t, 1:L // 2], e[:, t, L // 2 + 1:L]
                nc.gpsimd.tensor_tensor(pick[:, t, 1:L // 2], up, down, ALU.add).then_inc(w_folded, 1)
                nc.gpsimd.tensor_tensor(pick[:, t, L // 2 + 1:L], up, down, ALU.subtract).then_inc(w_folded, 1)
                nc.gpsimd.tensor_copy(pick[:, t, 0:L:L // 2], e[:, t, L // 2::-(L // 2)]).then_inc(w_folded, 1)

            nc.gpsimd.memset(zero[:], 0.0).then_inc(prod_added, 1)
            fold_v(0)
            shift_v(0)
            fold_q(0)

            def body(k, r, a, b, c, f):
                i = 4 * k + 2 + r
                if b:
                    for t in range(CT):
                        fold_w(i - 1, t)
                if a:
                    for n in range(4):
                        add_half(half_p(i, n), slot_p(i, n), ALU.add if n % 2 == 0 else ALU.subtract, None, None)
                        if n == 1:
                            twist_v(i, False)
                    if not b:
                        twist_v(i, True)
                if b:
                    for n in range(8):
                        blk = W_BLOCKS[n // 2]
                        dc_row = v_cyc[0:1, (r + 1) % 2, 0, :] if blk == 0 and n % 2 == 0 else None
                        add_half(half_r(i, n), slot_r(i, n), ALU.add if n % 2 == 0 else ALU.subtract, dc_row, i + 1)
                        if a and n == 3:
                            twist_v(i, True)
                if a:
                    pool.wait_ge(prod_ready, half_p(i, 3) + 1)
                    pool.wait_ge(last_scaled, i + 1)
                    nc.gpsimd.tensor_tensor(v_cyc[0:1, r % 2, 0, :], v_last[0:1, :], v_cyc[0:1, r % 2, 0, :],
                                            ALU.add).then_inc(dc_done, 1)
                late_norm = has_stats(k, r) and r == 1
                if f:
                    pool.wait_ge(evac_ready, evac_neg(i, 3) + 1)
                    fold_v(i + 1)
                    if not late_norm:
                        fold_q(i + 1)
                    shift_v(i + 1)
                if b:
                    pool.wait_ge(xr_loaded, 16 * i)
                    for h in range(2):
                        pool.wait_ge(even_copied, 2 * (i - 1) + h + 1)
                        nc.gpsimd.tensor_tensor(xr[:, h, :], rev[:, h, :], xr[:, h, :], ALU.add).then_inc(x2_step, 1)
                if late_norm:
                    fold_q(i + 1, False)

            steps(pool, body)


def ffn_phase(nc, sems, x2, a_w, b_w, wq_w, keys, tables, rstd2, shift2, out):
    with ExitStack() as st:
        def sb(name, shape, dt=F32):
            return st.enter_context(nc.sbuf_tensor(name, shape, dt))

        def ps(name, shape):
            return st.enter_context(nc.psum_tensor(name, shape, F32))

        def sem(name):
            return sems.enter_context(nc.semaphore(name))

        RING = 4
        a_hi, a_lo = sb("a_hi", [P, KD, NFFN], F32R), sb("a_lo", [P, KD, NFFN], F32R)
        b_hi, b_lo = sb("b_hi", [P, KN, D], F32R), sb("b_lo", [P, KN, D], F32R)
        wqk = sb("wqk", [P, KD, 2, EXPERTS], F32R)
        ident2, keys_sb, keys_t = sb("ident2", [P, P]), sb("keys_sb", [EXPERTS, RDIM]), sb("keys_t", [RDIM, EXPERTS])
        rows = [sb(f"rows{n}", [P, D]) for n in range(RING)]
        xn = sb("xn", [P, D])
        xt_hi, xt_lo = sb("xt_hi", [P, KD, P], F32R), sb("xt_lo", [P, KD, P], F32R)
        zg = sb("zg", [P, NFFN])
        zt_hi, zt_lo = sb("zt_hi", [P, KN, P], F32R), sb("zt_lo", [P, KN, P], F32R)
        best, best_neg, best_exp = sb("best", [P, TOPE]), sb("best_neg", [P, 1]), sb("best_exp", [P, TOPE])
        gate_sum, gate_inv = sb("gate_sum", [P, 1]), sb("gate_inv", [P, 1])
        scores, scores_lo = sb("scores", [P, EXPERTS]), sb("scores_lo", [P, EXPERTS])
        rest, score_exp, gate = sb("rest", [P, EXPERTS]), sb("score_exp", [P, EXPERTS]), sb("gate", [P, EXPERTS])
        pace2 = sb("pace2", [P, 32])

        tp_ps = [ps(f"tp{n}", [P, 4, P]) for n in range(2)]
        z4_ps, sc_ps, zt_ps = ps("z", [P, 4, P]), ps("score_sums", [P, NFFN]), ps("zt", [P, KN, P])
        out_ps = [ps(f"out{n}", [P, 512]) for n in range(2)]
        z_ps = z4_ps[:].rearrange("p m n -> p (m n)")
        stage_ps = [*tp_ps, z4_ps, zt_ps]

        small_loaded, out_stored = sem("small_loaded"), sem("out_stored")
        rows_loaded = [sem(f"rows_loaded{n}") for n in range(RING)]
        keys_turned, keys_copied, wqk_hi_done = sem("keys_turned"), sem("keys_copied"), sem("wqk_hi_done")
        xn_ready, tp_ready, tp_hi, tp_lo = sem("xn_ready"), sem("tp_ready"), sem("tp_hi"), sem("tp_lo")
        sc_ready, sc_summed, route_step, gate_exp = sem("sc_ready"), sem("sc_summed"), sem("route_step"), sem("gate_exp")
        gate_step, gate_ready = sem("gate_step"), sem("gate_ready")
        z_ready, zg_ready, zt_ready, zt_hi_done, zt_lo_done = (
            sem("z_ready"), sem("zg_ready"), sem("zt_ready"), sem("zt_hi_done"), sem("zt_lo_done"))
        out_ready, out_taken = sem("out_ready"), sem("out_taken")

        STAGES = 2 * KN
        x2_rows = x2.rearrange("b l d -> (b l) d").rearrange("(t p) d -> t p d", p=P)
        out_rows = out.rearrange("b l d -> (b l) d").rearrange("(t p) d -> t p d", p=P)
        b_rows = b_w.rearrange("(s t p) n -> s p t n", p=P, t=KN)

        def part_of_weights(w, s, q):
            a_t, b_t = w
            if s < KN:
                return a_t[:, 4 * q:4 * q + 4, s * P:(s + 1) * P]
            col = (4 * (s - KN) + q) * P
            return b_t[:, :, col:col + P]

        def tp_stage(s, q):
            return 4 * s + q

        def tp_tile(t, q):
            return 4 * (STAGES + t) + q

        def wait_rows(eng, k, n):
            eng.wait_ge(rows_loaded[n % RING], 16 * (k + n // RING + 1))

        def out_place(t, q):
            return 2 + 4 * t + q

        def steps(body):
            def run(eng):
                body(-1, 2, False, False, True)
                body(-1, 3, True, False, True)
                with eng.Fori(0, TT // RING - 1) as k:
                    for r in range(RING):
                        body(k, r, True, True, True)
                for r in range(RING):
                    body(TT // RING - 1, r, r < 3, True, r < 2)
            return run

        block = st.enter_context(nc.Block())

        @block.sync
        def _(sp):
            sp.dma_start(ident2[:], tables["ident"]).then_inc(small_loaded, 16)
            sp.dma_start(keys_sb[:], keys).then_inc(small_loaded, 16)
            for s in range(STAGES + RING):
                if s >= RING:
                    sp.wait_ge(tp_ready, tp_stage(s - RING, 3) + 1)
                buf = rows[s % RING]
                if s < KN:
                    sp.dma_start(buf[:], a_w[s * P:(s + 1) * P, :]).then_inc(rows_loaded[s % RING], 16)
                elif s < STAGES:
                    sp.dma_start(buf[:].rearrange("p (t n) -> p t n", t=KN), b_rows[s - KN]).then_inc(rows_loaded[s % RING], 16)
                else:
                    sp.dma_start(buf[:], x2_rows[s - STAGES]).then_inc(rows_loaded[s % RING], 16)
                if s == 0:
                    sp.dma_start(xn[0:RDIM, :], wq_w).then_inc(small_loaded, 16)

            def body(k, r, a, b, f):
                u = RING * k + 1 + r
                if b:
                    sp.wait_ge(out_taken, out_place(u - 1, 3) + 1)
                    sp.dma_start(out_rows[bass.ds(u - 1, 1)].rearrange("o p d -> (o p) d"), rows[r][:]).then_inc(out_stored, 16)
                if b and not isinstance(k, int):
                    sp.wait_ge(out_stored, 16 * u)
                    sp.dma_start(rows[r][:], x2_rows[bass.ds(u + 3, 1)].rearrange("o p d -> (o p) d")).then_inc(rows_loaded[r], 16)

            steps(body)(sp)
            sp.wait_ge(out_stored, 16 * TT)

        @block.tensor
        def _(pe):
            def split_mm(dst, lhs_hi, lhs_lo, rhs_hi, rhs_lo, start, stop):
                nc.tensor.matmul(dst, lhs_hi, rhs_hi, start=start, stop=False)
                nc.tensor.matmul(dst, lhs_hi, rhs_lo, start=False, stop=False)
                return nc.tensor.matmul(dst, lhs_lo, rhs_hi, start=False, stop=stop)

            def transposes(n, bank, ring, q, src):
                if not (isinstance(n, int) and n < ring):
                    pe.wait_ge(tp_lo, n - ring + 1)
                for m in range(4):
                    last = nc.tensor.transpose(bank[:, m, :], src[:, (4 * q + m) * P:(4 * q + m + 1) * P], ident2[:])
                last.then_inc(tp_ready, 1)

            pe.wait_ge(small_loaded, 16 * 3)
            nc.tensor.transpose(zt_ps[0:RDIM, 0, 0:EXPERTS], keys_sb[:], ident2[0:EXPERTS, 0:EXPERTS]).then_inc(keys_turned, 1)
            pe.wait_ge(keys_copied, 1)
            for h in range(2):
                for m in range(KD // 2):
                    kt = h * (KD // 2) + m
                    last = nc.tensor.matmul(out_ps[h][:, m * EXPERTS:(m + 1) * EXPERTS], xn[0:RDIM, kt * P:(kt + 1) * P],
                                            keys_t[:], start=True, stop=True)
                last.then_inc(out_ready, 1)
            for s in range(STAGES):
                wait_rows(pe, 0, s)
                for q in range(4):
                    transposes(tp_stage(s, q), stage_ps[q], 4, q, rows[s % RING])

            def body(k, r, a, b, f):
                u = RING * k + 1 + r
                if a:
                    pe.wait_ge(tp_hi, tp_tile(u, 3) + 1)
                    pe.wait_ge(tp_lo, tp_tile(u, 3) + 1)
                    if b:
                        pe.wait_ge(sc_summed, 2 * u)
                    else:
                        pe.wait_ge(wqk_hi_done, 2)
                        pe.wait_ge(out_taken, 2)
                    for kt in range(KD):
                        nc.tensor.matmul(sc_ps[:, 0:2 * EXPERTS], xt_hi[:, kt, :], wqk[:, kt, :, :].rearrange("p s e -> p (s e)"),
                                         start=kt == 0, stop=False)
                        last = nc.tensor.matmul(sc_ps[:, 0:EXPERTS], xt_lo[:, kt, :], wqk[:, kt, 0, :],
                                                start=False, stop=kt == KD - 1)
                    last.then_inc(sc_ready, 1)
                if b:
                    pe.wait_ge(zg_ready, u)
                    for m in range(KN):
                        last = nc.tensor.transpose(zt_ps[:, m, :], zg[:, m * P:(m + 1) * P], ident2[:])
                    last.then_inc(zt_ready, 1)
                if a:
                    for kt in range(KD):
                        last = split_mm(z_ps, xt_hi[:, kt, :], xt_lo[:, kt, :], a_hi[:, kt, :], a_lo[:, kt, :],
                                        kt == 0, kt == KD - 1)
                    last.then_inc(z_ready, 1)

                def tile_transposes(q):
                    if f:
                        if q == 0:
                            pe.wait_ge(xn_ready, u + 2)
                        transposes(tp_tile(u + 1, q), tp_ps[q % 2], 2, q, xn)

                def out_bank(q):
                    if b:
                        pe.wait_ge(out_taken, out_place(u - 1, q) - 1)
                        for m in range(KN):
                            cols = slice(q * 512, (q + 1) * 512)
                            last = split_mm(out_ps[q % 2][:], zt_hi[:, m, :], zt_lo[:, m, :],
                                            b_hi[:, m, cols], b_lo[:, m, cols], m == 0, m == KN - 1)
                        last.then_inc(out_ready, 1)

                tile_transposes(0)
                tile_transposes(1)
                if b:
                    pe.wait_ge(zt_hi_done, u)
                    pe.wait_ge(zt_lo_done, u)
                out_bank(0)
                tile_transposes(2)
                out_bank(1)
                tile_transposes(3)
                out_bank(2)
                out_bank(3)

            steps(body)(pe)

        @block.vector
        def _(dve):
            held = [0]

            def hold(sem_, value):
                dve.wait_ge(sem_, value)
                nc.vector.memset(pace2[:, held[0] % 32:held[0] % 32 + 1], 0.0)
                held[0] += 1

            def low(n, dst, hi, src):
                dve.wait_ge(tp_hi, n + 1)
                nc.vector.tensor_tensor(dst, src[:], hi.bitcast(F32), ALU.subtract).then_inc(tp_lo, 1)

            dve.wait_ge(keys_turned, 1)
            nc.vector.tensor_copy(keys_t[:], zt_ps[0:RDIM, 0, 0:EXPERTS]).then_inc(keys_copied, 1)
            for h in range(2):
                dve.wait_ge(wqk_hi_done, h + 1)
                part = slice(h * (KD // 2), (h + 1) * (KD // 2))
                nc.vector.tensor_tensor(wqk[:, part, 1, :], out_ps[h][:].rearrange("p (m e) -> p m e", e=EXPERTS),
                                        wqk[:, part, 0, :].bitcast(F32), ALU.subtract).then_inc(out_taken, 1)
            for s in range(STAGES):
                for q in range(4):
                    hi, lo = (part_of_weights(w, s, q) for w in ((a_hi, b_hi), (a_lo, b_lo)))
                    low(tp_stage(s, q), lo, hi, stage_ps[q])

            def body(k, r, a, b, f):
                u = RING * k + 1 + r
                if b:
                    dve.wait_ge(zt_hi_done, u)
                    nc.vector.tensor_tensor(zt_lo[:], zt_ps[:], zt_hi[:].bitcast(F32), ALU.subtract).then_inc(zt_lo_done, 1)
                if a:
                    dve.wait_ge(sc_ready, u + 1)
                    nc.vector.tensor_copy(scores_lo[:], sc_ps[:, EXPERTS:2 * EXPERTS]).then_inc(sc_summed, 1)
                    dve.wait_ge(sc_summed, 2 * u + 1)
                    nc.vector.tensor_tensor(scores[:], sc_ps[:, 0:EXPERTS], scores_lo[:], ALU.add).then_inc(sc_summed, 1)
                    hold(sc_summed, 2 * u + 2)
                    nc.vector.max(best[:, 0:8], scores[:]).then_inc(route_step, 1)
                    dve.wait_ge(route_step, 5 * u + 1)
                    nc.vector.tensor_scalar(best_neg[:], best[:, 0:1], -1.0, None, ALU.mult).then_inc(route_step, 1)
                    nc.vector.match_replace(rest[:], best[:, 0:8], scores[:], NEG).then_inc(route_step, 1)
                    hold(route_step, 5 * u + 3)
                    nc.vector.max(best[:, 8:16], rest[:]).then_inc(route_step, 1)
                    hold(route_step, 5 * u + 4)
                    nc.vector.match_replace(rest[:], best[:, 8:16], rest[:], NEG).then_inc(route_step, 1)
                    dve.wait_ge(gate_exp, 2 * u + 2)
                    nc.vector.reciprocal(gate_inv[:], gate_sum[:]).then_inc(gate_step, 1)
                    dve.wait_ge(gate_step, 2 * u + 1)
                    dve.wait_ge(route_step, 5 * u + 5)
                    nc.vector.tensor_scalar(gate[:], rest[:], NEG, gate_inv[:], ALU.is_equal, ALU.mult).then_inc(gate_step, 1)
                    dve.wait_ge(gate_step, 2 * u + 2)
                    nc.vector.tensor_tensor(gate[:], gate[:], score_exp[:], ALU.mult).then_inc(gate_ready, 1)
                    dve.wait_ge(gate_ready, u + 1)
                    dve.wait_ge(z_ready, u + 1)
                    if b:
                        dve.wait_ge(zt_ready, u)
                    nc.vector.tensor_tensor(zg[:].rearrange("p (e r) -> p e r", r=RANK),
                                            z_ps.rearrange("p (e r) -> p e r", r=RANK),
                                            gate[:].unsqueeze(2).broadcast_to((P, EXPERTS, RANK)), ALU.mult).then_inc(zg_ready, 1)

                def tile_low(q):
                    if f:
                        part = slice(4 * q, 4 * q + 4)
                        low(tp_tile(u + 1, q), xt_lo[:, part, :], xt_hi[:, part, :], tp_ps[q % 2])

                def add_out(q):
                    if b:
                        cols = slice(q * 512, (q + 1) * 512)
                        dve.wait_ge(out_ready, out_place(u - 1, q) + 1)
                        nc.vector.scalar_tensor_tensor(rows[r][:, cols], out_ps[q % 2][:], SCALING, rows[r][:, cols],
                                                       ALU.mult, ALU.add).then_inc(out_taken, 1)

                tile_low(0)
                tile_low(1)
                add_out(0)
                tile_low(2)
                add_out(1)
                tile_low(3)
                add_out(2)
                add_out(3)

            steps(body)(dve)

        @block.scalar
        def _(act):
            def high(n, dst, src):
                act.wait_ge(tp_ready, n + 1)
                nc.scalar.activation(dst, src[:], ACT.Copy).then_inc(tp_hi, 1)

            for h in range(2):
                act.wait_ge(out_ready, h + 1)
                nc.scalar.activation(wqk[:, h * (KD // 2):(h + 1) * (KD // 2), 0, :],
                                     out_ps[h][:].rearrange("p (m e) -> p m e", e=EXPERTS), ACT.Copy).then_inc(wqk_hi_done, 1)
            for s in range(STAGES):
                for q in range(4):
                    high(tp_stage(s, q), part_of_weights((a_hi, b_hi), s, q), stage_ps[q])
            wait_rows(act, 0, STAGES)

            def body(k, r, a, b, f):
                u = RING * k + 1 + r
                if f:
                    t = bass.ds(u + 1, 1)
                    nc.scalar.activation(xn[:], rows[(r + 2) % RING][:], ACT.Identity, bias=shift2[:, t],
                                         scale=rstd2[:, t]).then_inc(xn_ready, 1)
                if b:
                    act.wait_ge(zt_ready, u)
                    act.wait_ge(out_ready, out_place(u - 2, 3) + 1)
                    nc.scalar.activation(zt_hi[:], zt_ps[:], ACT.Copy).then_inc(zt_hi_done, 1)
                if a:
                    act.wait_ge(route_step, 5 * u + 3)
                    if b:
                        act.wait_ge(gate_ready, u)
                    nc.scalar.activation(score_exp[:], scores[:], ACT.Exp, bias=best_neg[:]).then_inc(gate_exp, 1)
                    act.wait_ge(route_step, 5 * u + 4)
                    nc.scalar.activation(best_exp[:], best[:], ACT.Exp, bias=best_neg[:], accum_out=gate_sum[:]).then_inc(gate_exp, 1)
                if f:
                    for q in range(4):
                        if q == 0 and a:
                            act.wait_ge(z_ready, u + 1)
                        if q == 3 and (u + 2 < TT if isinstance(u, int) else True):
                            wait_rows(act, k, STAGES + 3 + r)
                        high(tp_tile(u + 1, q), xt_hi[:, 4 * q:4 * q + 4, :], tp_ps[q % 2])

            steps(body)(act)


def build_program(nc, x, ctx, a_w, b_w, wq_w, keys, tables, out):
    with ExitStack() as sems, nc.sbuf_tensor("rstd2", [P, TT], F32) as rstd2, nc.sbuf_tensor("shift2", [P, TT], F32) as shift2:
        attention_phase(nc, sems, x, ctx, tables, out, rstd2, shift2)
        ffn_phase(nc, sems, out, a_w, b_w, wq_w, keys, tables, rstd2, shift2, out)


_INS = ["x", "ctx_4096", "L0_ffn_A_w", "L0_ffn_B_w", "L0_ffn_Wq_w", "L0_ffn_keys"]


def kernel(**inputs):
    import numpy as _np
    import concourse.bacc as _bacc
    from concourse import mybir as _mybir
    from concourse.bass_utils import run_bass_kernel_spmd as _run

    nc = _bacc.Bacc("TRN2", target_bir_lowering=False, num_devices=1)
    arrays, args, tabs = {}, [], {}
    for name in _INS:
        a = _np.ascontiguousarray(inputs[name])
        arrays[f"in_{name}_dram"] = a
        args.append(nc.dram_tensor(f"in_{name}_dram", a.shape, _mybir.dt.from_np(a.dtype), kind="ExternalInput").ap())
    for name, a in transform_tables().items():
        arrays[f"table_{name}_dram"] = a
        tabs[name] = nc.dram_tensor(f"table_{name}_dram", a.shape, _mybir.dt.float32, kind="ExternalInput").ap()
    out = nc.dram_tensor("out_0_dram", (B, L, D), _mybir.dt.float32, kind="ExternalOutput").ap()
    build_program(nc, *args, tabs, out)
    r = _run(nc, [arrays], core_ids=[0])
    return r.results[0]["out_0_dram"]
```
